# Optimizing a Trainium2 kernel written in Bass

```python
import numpy as np
import jax
import jax.numpy as jnp

def _softmax(x, axis=-1):
    return jax.nn.softmax(x, axis=axis)

def _gelu(x):
    return jax.nn.gelu(x, approximate=True)

def _silu(x):
    return jax.nn.silu(x)

def _sigmoid(x):
    return jax.nn.sigmoid(x)

def _layernorm(x, axis=-1, eps=1e-05):
    m = jnp.mean(x, axis=axis, keepdims=True)
    v = jnp.var(x, axis=axis, keepdims=True)
    return (x - m) / jnp.sqrt(v + eps)

def _scatter_add(tgt, idx, src, axis=0):
    return tgt.at[idx].add(src)

def _segment_sum(src, seg, n):
    return jax.ops.segment_sum(src, seg, n)
kernel_name = 'mk_xattn_ffn_d1_seqx_r8_e380bb'

def setup_inputs(seed: int=0):
    np.random.seed(seed)
    _w = jnp.asarray

    def _rec_inputs():
        import jax
        import jax.numpy as jnp
        _rk = jax.random.key(seed)
        x = -0.0003929 + 0.9999 * jax.random.normal(jax.random.fold_in(_rk, 1), (8, 256, 128), jnp.float32)
        _lenS = 256 - jax.random.randint(jax.random.fold_in(_rk, 7), (8,), 0, max(1, 256 // 4) + 1, jnp.int32)
        _lenS2 = 64 - jax.random.randint(jax.random.fold_in(_rk, 8), (8,), 0, max(1, 64 // 4) + 1, jnp.int32)
        _ctx_512P = jax.random.normal(jax.random.fold_in(_rk, 11), (8, 16, 64), jnp.float32)
        _ctx_512c = jax.random.dirichlet(jax.random.fold_in(_rk, 511), 0.3 * jnp.ones((16,), jnp.float32), (8, 64))
        _ctx_512t = jnp.einsum('bsk,bkd->bsd', _ctx_512c, _ctx_512P)
        _ctx_512t = _ctx_512t * jax.lax.rsqrt(jnp.mean(jnp.square(_ctx_512t)) + 1e-12) * 0.953939
        ctx_512 = -1.39393e-06 + 0.999914 * (_ctx_512t + 0.3 * jax.random.normal(jax.random.fold_in(_rk, 611), (8, 64, 64), jnp.float32))
        return (x, ctx_512)
    x, ctx_512 = _rec_inputs()

    def _L0_xattn_setup():
        import jax, jax.numpy as jnp
        import numpy as np
        HEADS = 16
        D_MODEL = 128
        IMG_MODEL = 64
        D_K = D_MODEL // HEADS
        key = jax.random.key(seed)
        ks = jax.random.split(key, 12)
        B, LQ, LKV = (8, 256, 128)
        s_dm = 1.0 / np.sqrt(D_MODEL)
        s_im = 1.0 / np.sqrt(IMG_MODEL)
        return {'q': jax.random.normal(ks[0], (B, LQ, D_MODEL), jnp.float32), 'k': jax.random.normal(ks[1], (B, LKV, IMG_MODEL), jnp.float32), 'v': jax.random.normal(ks[2], (B, LKV, IMG_MODEL), jnp.float32), 'Wq': jax.random.normal(ks[3], (D_MODEL, D_MODEL), jnp.float32) * s_dm, 'bq': jnp.zeros((D_MODEL,), jnp.float32), 'Wk': jax.random.normal(ks[4], (IMG_MODEL, D_MODEL), jnp.float32) * s_im, 'bk': jnp.zeros((D_MODEL,), jnp.float32), 'Wv': jax.random.normal(ks[5], (IMG_MODEL, D_MODEL), jnp.float32) * s_im, 'bv': jnp.zeros((D_MODEL,), jnp.float32), 'Wo': jax.random.normal(ks[6], (D_MODEL, D_MODEL), jnp.float32) * s_dm, 'bo': jnp.zeros((D_MODEL,), jnp.float32)}
    _L0_xattn_all = _L0_xattn_setup()
    _L0_xattn_in = {k: v for k, v in _L0_xattn_all.items() if k in ('Wq', 'bq', 'Wk', 'bk', 'Wv', 'bv', 'Wo', 'bo')}
    del _L0_xattn_all

    def _L0_ffn_setup():
        import jax, jax.numpy as jnp
        import numpy as np
        NUM_EXPERTS = 8
        HIDDEN = 128
        FFN = 512
        BATCH = 2
        SEQ = 256
        key = jax.random.key(seed)
        k_x, k_g, k_u, k_d = jax.random.split(key, 4)
        scale_in = 1.0 / np.sqrt(HIDDEN)
        scale_mid = 1.0 / np.sqrt(FFN)
        return {'hidden_states': jax.random.normal(k_x, (BATCH, SEQ, HIDDEN), dtype=jnp.float32), 'Wg': jax.random.normal(k_g, (NUM_EXPERTS, HIDDEN, FFN), dtype=jnp.float32) * scale_in, 'Wu': jax.random.normal(k_u, (NUM_EXPERTS, HIDDEN, FFN), dtype=jnp.float32) * scale_in, 'Wd': jax.random.normal(k_d, (NUM_EXPERTS, FFN, HIDDEN), dtype=jnp.float32) * scale_mid}
    _L0_ffn_all = _L0_ffn_setup()
    _L0_ffn_in = {k: v for k, v in _L0_ffn_all.items() if k in ('Wg', 'Wu', 'Wd')}
    del _L0_ffn_all
    return {'x': x, 'ctx_512': ctx_512, 'L0_xattn_Wq': _L0_xattn_in['Wq'], 'L0_xattn_bq': _L0_xattn_in['bq'], 'L0_xattn_Wk': _L0_xattn_in['Wk'], 'L0_xattn_bk': _L0_xattn_in['bk'], 'L0_xattn_Wv': _L0_xattn_in['Wv'], 'L0_xattn_bv': _L0_xattn_in['bv'], 'L0_xattn_Wo': _L0_xattn_in['Wo'], 'L0_xattn_bo': _L0_xattn_in['bo'], 'L0_ffn_Wg': _L0_ffn_in['Wg'], 'L0_ffn_Wu': _L0_ffn_in['Wu'], 'L0_ffn_Wd': _L0_ffn_in['Wd']}

def reference(x, ctx_512, L0_xattn_Wq, L0_xattn_bq, L0_xattn_Wk, L0_xattn_bk, L0_xattn_Wv, L0_xattn_bv, L0_xattn_Wo, L0_xattn_bo, L0_ffn_Wg, L0_ffn_Wu, L0_ffn_Wd):
    import jax
    import jax.numpy as jnp

    def _L0_xattn_ref(q, k, v, Wq, bq, Wk, bk, Wv, bv, Wo, bo):
        import jax, jax.numpy as jnp
        import numpy as np
        HEADS = 16
        D_MODEL = 128
        IMG_MODEL = 64
        D_K = D_MODEL // HEADS
        B, LQ, _ = q.shape
        LKV = k.shape[1]
        qh = (q @ Wq + bq).reshape(B, LQ, HEADS, D_K).transpose(0, 2, 1, 3)
        kh = (k @ Wk + bk).reshape(B, LKV, HEADS, D_K).transpose(0, 2, 1, 3)
        vh = (v @ Wv + bv).reshape(B, LKV, HEADS, D_K).transpose(0, 2, 1, 3)
        scale = 1.0 / np.sqrt(D_K)
        scores = jnp.einsum('bhqd,bhkd->bhqk', qh, kh) * scale
        attn = jax.nn.softmax(scores, axis=-1)
        out = jnp.einsum('bhqk,bhkd->bhqd', attn, vh)
        concat = out.transpose(0, 2, 1, 3).reshape(B, LQ, D_MODEL)
        return concat @ Wo + bo

    def _L0_ffn_ref(hidden_states, Wg, Wu, Wd):
        import jax, jax.numpy as jnp
        import numpy as np
        NUM_EXPERTS = 8
        HIDDEN = 128
        FFN = 512
        BATCH = 2
        SEQ = 256
        B, S, H = hidden_states.shape
        x = hidden_states.reshape(-1, H)

        def expert_step(acc, w):
            wg, wu, wd = w
            h = jax.nn.silu(x @ wg) * (x @ wu)
            return (acc + h @ wd, None)
        acc, _ = jax.lax.scan(expert_step, jnp.zeros_like(x), (Wg, Wu, Wd))
        return acc.reshape(B, S, H)
    x = x + _L0_xattn_ref(_layernorm(x, axis=-1), ctx_512, ctx_512, L0_xattn_Wq, L0_xattn_bq, L0_xattn_Wk, L0_xattn_bk, L0_xattn_Wv, L0_xattn_bv, L0_xattn_Wo, L0_xattn_bo)
    x = x + _L0_ffn_ref(_layernorm(x, axis=-1), L0_ffn_Wg, L0_ffn_Wu, L0_ffn_Wd)
    return x

_drawn_inputs = setup_inputs


def setup_inputs(seed=0):
    import zlib

    import numpy as np

    out = dict(_drawn_inputs(seed))
    spreads = {'L0_xattn_bq': (0.0, 0.1),
     'L0_xattn_bk': (0.0, 0.1),
     'L0_xattn_bv': (0.0, 0.1),
     'L0_xattn_bo': (0.0, 0.1)}
    factors = {}
    for name, (base, spread) in spreads.items():
        noise = np.random.default_rng([zlib.crc32(name.encode()), seed]).standard_normal(out[name].shape)
        drawn = base * np.exp(spread * noise) if base else spread * noise
        out[name] = jnp.asarray(drawn.astype(out[name].dtype))
    for name, factor in factors.items():
        out[name] = (out[name] * factor).astype(out[name].dtype)
    return out
```

```python
from contextlib import ExitStack

import concourse.bass as bass
from concourse import mybir
from concourse.alu_op_type import AluOpType as ALU

F32 = mybir.dt.float32
BF16 = mybir.dt.bfloat16
F16 = mybir.dt.float16
I32 = mybir.dt.int32
ACT = mybir.ActivationFunctionType
AX = mybir.AxisListType

P = 128
EPS = 1e-5
X_SCALE = 256.0
W_TOP = 2.0 ** 13


def build(nc, x, ctx_in, Wq, bq, Wk, bk, Wv, bv, Wo, bo, Wg, Wu, Wd, out):
    B, LQ, D = x.shape
    _, LK, DC = ctx_in.shape
    E, _, F = Wg.shape
    H = 16
    DH = D // H
    SCALE = float(DH) ** -0.5
    T = LQ // P
    NT = B * T
    R = 4
    J = H // R
    PAIRS = H // 2
    VC = 2 * DH + 2
    CB = 512 // LQ
    NC = B // CB
    CH = CB * LQ
    FT = F // P
    WE = FT * P
    KT_TILES = B * LK // P
    assert D == P and 2 * LK == P and FT == 4 and CH == 512 and NT == 16

    with ExitStack() as es:
        def sb(name, shape, dt=F32):
            return es.enter_context(nc.sbuf_tensor(name, shape, dt))

        def sem(name):
            return es.enter_context(nc.semaphore(name))

        x_sb = sb("x_sb", [P, NT, D])
        ctx_sb = sb("ctx_sb", [P, KT_TILES, DC])
        wq_sb = sb("wq_sb", [P, D])
        wk_sb = sb("wk_sb", [DC + 1, D])
        wv_sb = sb("wv_sb", [DC + 1, D])
        wo_sb = sb("wo_sb", [P, D])
        bq_sb = sb("bq_sb", [P, 1])
        bo_sb = sb("bo_sb", [P, D])
        w32 = [sb(f"w32_{n}", [P, E, WE]) for n in ("gate", "up", "down")]
        whi = [sb(f"whi_{n}", [P, E, WE], F16) for n in ("gate", "up", "down")]
        wlo = [sb(f"wlo_{n}", [P, E, WE], F16) for n in ("gate", "up", "down")]
        ident = sb("ident", [P, P])
        ident16 = sb("ident16", [P, P], BF16)
        head_mask = sb("head_mask", [P, J])
        mod_mask = sb("mod_mask", [P, J])
        max_sel = sb("max_sel", [P, J, LK], BF16)
        ones3 = sb("ones3", [P, P])
        eps_c = sb("eps_c", [P, 1])
        half_c = sb("half_c", [P, NT])
        bqs = sb("bqs", [P, 1])
        stats = sb("stats", [P, NT, 6])
        mv = sb("mv", [P, NT, 2])
        rstd = sb("rstd", [P, NT])
        vare = sb("vare", [P, NT])
        xn = sb("xn", [P, NT, D])
        xnT = sb("xnT", [P, NT * P])
        xbo = x_sb
        x1 = x_sb
        xh = sb("xh", [P, NC, CH], F16)
        xl = sb("xl", [P, NC, CH], F16)
        ctxT = sb("ctxT", [DC + 1, B, 2, LK])
        kT = sb("kT", [P, B, LK])
        v_op = sb("v_op", [P, B, PAIRS, VC])
        qT = [sb(f"qT{i}", [P, LQ]) for i in range(2)]
        k_op = [sb(f"k_op{i}", [P, J, LK]) for i in range(2)]
        nmax = [sb(f"nmax{i}", [P, R, T, J]) for i in range(2)]
        nmax_parts = [sb(f"nmax_parts{i}", [P, T, R, 32], BF16) for i in range(2)]
        nmaxT = [sb(f"nmaxT{i}", [P, LQ], BF16) for i in range(2)]
        prob = [sb(f"prob{i}", [P, PAIRS, LQ]) for i in range(2)]
        rsum = [sb(f"rsum{i}", [P, T, PAIRS, 2]) for i in range(2)]
        o_sb = [sb(f"o_sb{i}", [P, T, H, DH]) for i in range(2)]
        oT = [sb(f"oT{i}", [P, LQ]) for i in range(2)]
        wmax = sb("wmax", [P, 3])
        wmaxd = sb("wmaxd", [3, 4])
        wexp = sb("wexp", [P, 3])
        wscale = sb("wscale", [P, 3])
        fac = sb("fac", [P, 8])
        sg = [sb(f"sg{i}", [P, CH]) for i in range(4)]
        h32 = [sb(f"h32_{i}", [P, CH]) for i in range(4)]
        hh = [sb(f"hh{i}", [P, CH], F16) for i in range(4)]
        hl = [sb(f"hl{i}", [P, CH], F16) for i in range(4)]
        yT = sb("yT", [P, CH])
        y_sb = [sb(f"y_sb{i}", [P, CH]) for i in range(2)]

        ps = es.enter_context(nc.psum_tensor("ps", [P, 8, 512], F32))

        s_x = [sem(f"x_loaded{c}") for c in range(NC)]
        s_ctx, s_wq, s_small = sem("ctx_loaded"), sem("wq_loaded"), sem("small_loaded")
        s_w = sem("ffn_weights_loaded")
        s_cst, s_ident = sem("constants_set"), sem("identity_set")
        s_vset = sem("value_columns_set")
        s_mask, s_sel = sem("masks_set"), sem("max_sel_set")
        s_ctxT_ps, s_ctxT = sem("ctxT_in_psum"), sem("ctxT_copied")
        s_kv_ps, s_kT, s_v = sem("kv_in_psum"), sem("kT_copied"), sem("v_copied")
        s_bqs = sem("bq_scaled")
        s_st, s_mv, s_ve, s_rstd, s_xn = sem("ln1_stats"), sem("ln1_mean_var"), sem("ln1_var_eps"), sem("ln1_rstd"), sem("ln1_rows")
        s_xnT_ps, s_xnT, s_xbo = sem("xnT_in_psum"), sem("xnT_copied"), sem("x_plus_bo")
        s_q_ps, s_qT, s_kop = sem("q_in_psum"), sem("qT_ready"), sem("k_operand_ready")
        s_s_ps, s_nm, s_nmh, s_nml = sem("scores_in_psum"), sem("max_ready"), sem("max_hi"), sem("max_parts")
        s_nmT_ps, s_nmT = sem("maxT_in_psum"), sem("maxT_copied")
        s_st_ps, s_p = sem("scoresT_in_psum"), sem("prob_ready")
        s_o_ps, s_rs, s_o = sem("out_in_psum"), sem("sums_inverted"), sem("out_normed")
        s_oT_ps, s_oT, s_wo_ps, s_x1 = sem("oT_in_psum"), sem("oT_copied"), sem("wo_in_psum"), sem("x1_ready")
        s_wmax, s_wmT_ps, s_wm1, s_wd = sem("weight_max"), sem("weight_maxT_in_psum"), sem("weight_max_all"), sem("weight_max_diag")
        s_wb_ps, s_fac = sem("weight_max_in_psum"), sem("factors")
        s_ws, s_wh, s_wl = sem("weights_scaled"), sem("weights_hi"), sem("weights_lo")
        s_st2, s_mv2, s_ve2, s_rstd2, s_xn2 = sem("ln2_stats"), sem("ln2_mean_var"), sem("ln2_var_eps"), sem("ln2_rstd"), sem("ln2_rows")
        s_x2_ps, s_xh, s_xl = sem("x2T_in_psum"), sem("x2T_hi"), sem("x2T_lo")
        s_g, s_u, s_sg, s_h, s_hh, s_hl, s_d = (sem("gate_in_psum"), sem("up_in_psum"), sem("silu_ready"), sem("h_ready"),
                                                sem("h_hi"), sem("h_lo"), sem("down_added"))
        s_yT, s_y_ps, s_y, s_out = sem("yT_ready"), sem("y_in_psum"), sem("y_ready"), [sem(f"rows_stored{i}") for i in range(2)]

        x_view = x.rearrange("b (p t) d -> p b t d", t=T)
        out_view = out.rearrange("b (p t) d -> p b t d", t=T)
        x_by_b = x_sb[:, :, :].rearrange("p (b t) d -> p b t d", t=T)
        c_view = ctx_in.rearrange("(n m) k d -> (m k) n d", n=KT_TILES)
        w_view = [Wg.rearrange("e p f -> p e f"), Wu.rearrange("e p f -> p e f"),
                  Wd.rearrange("e (t p) d -> p e t d", p=P)]

        block = es.enter_context(nc.Block())

        @block.sync
        def _(sp):
            for c in range(NC):
                sp.dma_start(x_by_b[:, CB * c:CB * c + CB], x_view[:, CB * c:CB * c + CB]).then_inc(s_x[c], 16)
                if c == 0:
                    sp.dma_start(wq_sb[:, :], Wq).then_inc(s_wq, 16)
            sp.dma_start(wo_sb[:, :], Wo).then_inc(s_wq, 16)
            for e in range(0, E, 2):
                for m in range(3):
                    dst = w32[m][:, e:e + 2, :]
                    if m == 2:
                        dst = dst.rearrange("p e (t d) -> p e t d", t=FT)
                    sp.dma_start(dst, w_view[m][:, e:e + 2]).then_inc(s_w, 16)
            for c in range(NC):
                sp.wait_ge(s_y, c + 1)
                sp.dma_start(out_view[:, CB * c:CB * c + CB],
                             y_sb[c % 2][:, :].rearrange("p (b t d) -> p b t d", b=CB, t=T)).then_inc(s_out[c % 2], 16)
            for i in range(2):
                sp.wait_ge(s_out[i], 16 * NC // 2)

        @block.gpsimd
        def _(pool):
            pool.memset(ident[:, :], 0.0).then_inc(s_cst, 1)
            pool.wait_ge(s_cst, 1)
            pool.affine_select(out=ident[:, :], in_=ident[:, :], compare_op=ALU.not_equal, fill=1.0, base=0,
                               pattern=[[-1, P]], channel_multiplier=1).then_inc(s_ident, 1)
            pool.memset(half_c[:, :], -0.5).then_inc(s_cst, 1)
            pool.memset(ones3[:, :], 1.0).then_inc(s_cst, 1)
            for i in range(2):
                pool.memset(nmax_parts[i][:, :, :, :], 0.0).then_inc(s_cst, 1)
            pool.wait_ge(s_ident, 1)
            pool.tensor_copy(ident16[:, :], ident[:, :]).then_inc(s_ident, 1)
            pool.wait_ge(s_ve, 1)
            pool.wait_ge(s_cst, 5)
            pool.tensor_tensor(rstd[:, :], vare[:, :], half_c[:, :], ALU.pow).then_inc(s_rstd, 1)
            pool.wait_ge(s_xn, NT)
            pool.wait_ge(s_small, 16 * 6)
            pool.tensor_tensor(xbo[:, :, :], x_sb[:, :, :], bo_sb[:, :].unsqueeze(1).to_broadcast([P, NT, D]),
                               ALU.add).then_inc(s_xbo, 1)
            pool.wait_ge(s_mask, 1)
            pool.wait_ge(s_kT, 1)

            def key_operand(b, i, reuse):
                if reuse:
                    pool.wait_ge(s_st_ps, b - 1)
                pool.tensor_tensor(k_op[i][:, :, :],
                                   kT[:, bass.ds(b, 1), :].to_broadcast([P, J, LK]),
                                   head_mask[:, :].unsqueeze(2).to_broadcast([P, J, LK]), ALU.mult).then_inc(s_kop, 1)

            key_operand(0, 0, False)
            key_operand(1, 1, False)
            with pool.Fori(0, B // 2 - 1) as n:
                key_operand(n * 2 + 2, 0, True)
                key_operand(n * 2 + 3, 1, True)

            with pool.Fori(0, NC) as c:
                pool.wait_ge(s_ve2, c + 1)
                pool.tensor_tensor(rstd[:, bass.ds(c * 4, 4)], vare[:, bass.ds(c * 4, 4)], half_c[:, 0:4],
                                   ALU.pow).then_inc(s_rstd2, 1)

            pool.wait_ge(s_fac, 1)
            for e in range(E):
                for m in range(3):
                    w = w32[m][:, e, :]
                    pool.tensor_scalar(w, w, wscale[:, m:m + 1], None, ALU.mult).then_inc(s_ws, 1)
                for m in range(3):
                    w = w32[m][:, e, :]
                    pool.wait_ge(s_wh, e * 3 + (m + 1))
                    pool.tensor_tensor(wlo[m][:, e, :], w, whi[m][:, e, :],
                                       ALU.subtract).then_inc(s_wl, 1)

        @block.scalar
        def _(act):
            for n in range(KT_TILES):
                pass
            act.dma_start(ctx_sb[:, :, :], c_view).then_inc(s_ctx, 16)
            act.dma_start(wk_sb[0:DC, :], Wk).then_inc(s_small, 16)
            act.dma_start(wk_sb[DC:DC + 1, :], bk.rearrange("(a d) -> a d", a=1)).then_inc(s_small, 16)
            act.dma_start(wv_sb[0:DC, :], Wv).then_inc(s_small, 16)
            act.dma_start(wv_sb[DC:DC + 1, :], bv.rearrange("(a d) -> a d", a=1)).then_inc(s_small, 16)
            act.dma_start(bq_sb[:, :], bq.rearrange("(d a) -> d a", a=1)).then_inc(s_small, 16)
            act.dma_start(bo_sb[:, :], bo.partition_broadcast(P)).then_inc(s_small, 16)
            act.wait_ge(s_small, 16 * 6)
            nc.scalar.mul(bqs[:, :], bq_sb[:, :], SCALE).then_inc(s_bqs, 1)
            act.wait_ge(s_ctxT_ps, 1)
            for m in range(2):
                nc.scalar.copy(ctxT[0:DC, :, m, :], ps[0:DC, 0, :].rearrange("p (b k) -> p b k", k=LK)).then_inc(s_ctxT, 1)
            act.wait_ge(s_kv_ps, 1)
            nc.scalar.copy(kT[:, :, :], ps[:, 1, :].rearrange("p (b k) -> p b k", k=LK)).then_inc(s_kT, 1)
            act.wait_ge(s_kv_ps, 2)
            act.wait_ge(s_vset, 4)
            for n in range(2):
                for j in range(2):
                    half = slice(LK * j, LK * j + LK)
                    for g in range(4):
                        b = 4 * n + g
                        nc.scalar.copy(v_op[half, b, :, DH * j:DH * j + DH],
                                       ps[half, 2 + n, P * g:P * g + P].rearrange("p (r j d) -> p r j d", j=2, d=DH)[:, :, j, :]
                                       ).then_inc(s_v, 1)
            for c in range(NC):
                act.wait_ge(s_xnT_ps, c + 1)
                nc.scalar.copy(xnT[:, CH * c:CH * c + CH], ps[:, 4 + c, :]).then_inc(s_xnT, 1)
            act.wait_ge(s_bqs, 1)

            def first(b, i, reuse):
                g = 4 * i
                act.wait_ge(s_q_ps, b + 1)
                if reuse:
                    act.wait_ge(s_st_ps, b - 1)
                nc.scalar.activation(qT[i][:, :], ps[:, g, 0:LQ], ACT.Identity, bias=bqs[:, 0:1], scale=SCALE).then_inc(s_qT, 1)
                act.wait_ge(s_nmT_ps, b + 1)
                nc.scalar.copy(nmaxT[i][:, :], ps[:, g, 0:P].bitcast(BF16)).then_inc(s_nmT, 1)
                act.wait_ge(s_st_ps, b + 1)
                if reuse:
                    act.wait_ge(s_o_ps, b - 1)
                for a in range(2):
                    nc.scalar.activation(prob[i][:, 4 * a:4 * a + 4, :],
                                         ps[:, g + 2 * a:g + 2 * a + 2, :].rearrange("p r (t q) -> p (r t) q", t=2),
                                         ACT.Exp).then_inc(s_p, 1)

            def second(b, i):
                act.wait_ge(s_oT_ps, b + 1)
                nc.scalar.copy(oT[i][:, :], ps[:, 4 * i + 1, 0:LQ]).then_inc(s_oT, 1)

            first(0, 0, False)
            first(1, 1, False)
            second(0, 0)
            with act.Fori(0, B // 2 - 1) as n:
                first(n * 2 + 2, 0, True)
                second(n * 2 + 1, 1)
                first(n * 2 + 3, 1, True)
                second(n * 2 + 2, 0)
            second(B - 1, 1)

            with act.Fori(0, NC) as c:
                act.wait_ge(s_x2_ps, c + 1)
                nc.scalar.activation(xh[:, bass.ds(c, 1), :], ps[:, 5, :].unsqueeze(1), ACT.Copy, scale=X_SCALE).then_inc(s_xh, 1)

            def weights(e):
                for m in range(3):
                    act.wait_ge(s_ws, e * 3 + (m + 1))
                    nc.scalar.copy(whi[m][:, bass.ds(e, 1), :], w32[m][:, bass.ds(e, 1), :]).then_inc(s_wh, 1)

            act.wait_ge(s_fac, 1)
            for e in range(2):
                weights(e)

            def silu(i, u):
                act.wait_ge(s_g, i + 1)
                nc.scalar.activation(sg[u % 4][:, :], ps[:, u % 2, :], ACT.Silu, scale=fac[:, 0:1]).then_inc(s_sg, 1)

            def high(i, u):
                act.wait_ge(s_h, i + 1)
                nc.scalar.copy(hh[u % 4][:, :], h32[u % 4][:, :]).then_inc(s_hh, 1)

            def body(e, first):
                for u in range(FT):
                    i = e * FT + u
                    if not (first and u < 4):
                        act.wait_ge(s_h, i - 3)
                    silu(i, u)
                    if not (first and u == 0):
                        if not (first and u <= 4):
                            act.wait_ge(s_d, i - 4)
                        high(i - 1, (u - 1) % 4)

            body(0, True)
            with act.Fori(1, 4) as e:
                body(e, False)
                weights(e * 2)
                weights(e * 2 + 1)
            with act.Fori(4, NC * E) as e:
                body(e, False)
            act.wait_ge(s_d, NC * E * FT - 4)
            high(NC * E * FT - 1, 3)

        @block.vector
        def _(dve):
            nc.vector.memset(v_op[:, :, :, :], 0.0).then_inc(s_vset, 1)
            nc.vector.memset(ctxT[DC:DC + 1, :, :, :], 1.0).then_inc(s_vset, 1)
            dve.wait_ge(s_vset, 1)
            for j in range(2):
                nc.vector.memset(v_op[LK * j:LK * j + LK, :, :, 2 * DH + j], 1.0).then_inc(s_vset, 1)
            dve.wait_ge(s_ident, 1)
            nc.vector.tensor_reduce(head_mask[:, :], ident[:, :].rearrange("p (a j d) -> p j a d", j=J, d=DH), AX.XY, ALU.add).then_inc(s_mask, 1)
            nc.vector.tensor_reduce(mod_mask[:, :], ident[:, :].rearrange("p (n c) -> p c n", c=J), AX.X, ALU.add).then_inc(s_mask, 1)
            dve.wait_ge(s_mask, 2)
            nc.vector.tensor_copy(max_sel[:, :, :], mod_mask[:, :].unsqueeze(2).to_broadcast([P, J, LK])).then_inc(s_sel, 1)
            for c in range(NC):
                dve.wait_ge(s_x[c], 16)
                for t in range(4 * c, 4 * c + 4):
                    nc.vector.bn_stats(stats[:, t, :], x_sb[:, t, :]).then_inc(s_st, 1)
            for t in range(NT):
                dve.wait_ge(s_st, t + 1)
                nc.vector.bn_aggr(mv[:, t, :], stats[:, t, :]).then_inc(s_mv, 1)
            dve.wait_ge(s_mv, NT)
            nc.vector.tensor_scalar(vare[:, :], mv[:, :, 1], EPS, None, ALU.add).then_inc(s_ve, 1)
            dve.wait_ge(s_rstd, 1)
            for t in range(NT):
                nc.vector.tensor_scalar(xn[:, t, :], x_sb[:, t, :], mv[:, t, 0:1], rstd[:, t:t + 1], ALU.subtract, ALU.mult).then_inc(s_xn, 1)
            dve.wait_ge(s_cst, 5)
            dve.wait_ge(s_xbo, 1)

            def first(b, i):
                g = 4 * i
                dve.wait_ge(s_s_ps, b + 1)
                nc.vector.tensor_reduce(nmax[i][:, :, :, :], ps[:, g:g + 4, :].rearrange("p r (t j k) -> p (r t j) k", t=T, j=J),
                                        AX.X, ALU.max, negate=True).then_inc(s_nm, 1)
                dve.wait_ge(s_nm, b + 1)
                hi = nmax_parts[i][:, :, :, 0:J].rearrange("p t r j -> p r t j")
                lo = nmax_parts[i][:, :, :, J:2 * J].rearrange("p t r j -> p r t j")
                nc.vector.tensor_copy(hi, nmax[i][:, :, :, :]).then_inc(s_nmh, 1)
                dve.wait_ge(s_nmh, b + 1)
                nc.vector.tensor_tensor(lo, nmax[i][:, :, :, :], hi, ALU.subtract).then_inc(s_nml, 1)

            def second(b, i):
                g = 4 * i
                dve.wait_ge(s_o_ps, b + 1)
                o_ps = ps[:, g, 0:T * PAIRS * VC].rearrange("p (t r c) -> p t r c", t=T, c=VC)
                nc.vector.reciprocal(rsum[i][:, :, :, :], o_ps[:, :, :, 2 * DH:VC]).then_inc(s_rs, 1)
                dve.wait_ge(s_rs, b + 1)
                for t in range(T):
                    nc.vector.tensor_tensor(o_sb[i][:, t, :, :].rearrange("p (r j) d -> p r j d", j=2),
                                            o_ps[:, t, :, 0:2 * DH].rearrange("p r (j d) -> p r j d", j=2),
                                            rsum[i][:, t, :, :].unsqueeze(3).to_broadcast([P, PAIRS, 2, DH]), ALU.mult).then_inc(s_o, 1)
                dve.wait_ge(s_wo_ps, b + 1)
                nc.vector.tensor_tensor(x1[:, bass.ds(b * T, T), :], ps[:, g + 2, 0:LQ].rearrange("p (t d) -> p t d", t=T),
                                        xbo[:, bass.ds(b * T, T), :], ALU.add).then_inc(s_x1, 1)

            first(0, 0)
            with dve.Fori(0, B // 2 - 1) as n:
                first(n * 2 + 1, 1)
                second(n * 2, 0)
                first(n * 2 + 2, 0)
                second(n * 2 + 1, 1)
            first(B - 1, 1)
            second(B - 2, 0)
            dve.wait_ge(s_w, 16 * 3 * E // 2)
            for m in range(3):
                nc.vector.tensor_reduce(wmax[:, m:m + 1], w32[m][:, :, :], AX.XY, ALU.max, apply_absolute_value=True).then_inc(s_wmax, 1)
            second(B - 1, 1)
            dve.wait_ge(s_wmT_ps, 1)
            nc.vector.tensor_reduce(wmaxd[:, 3:4], ps[0:3, 7, 0:P], AX.X, ALU.max).then_inc(s_wm1, 1)
            dve.wait_ge(s_wm1, 1)
            nc.vector.tensor_scalar(wmaxd[:, 0:3], ident[0:3, 0:3], wmaxd[:, 3:4], None, ALU.mult).then_inc(s_wd, 1)
            dve.wait_ge(s_wb_ps, 1)
            nc.vector.tensor_scalar(wmax[:, :], ps[:, 6, 0:3], 1e-30, 1e30, ALU.max, ALU.min).then_inc(s_wm1, 1)
            dve.wait_ge(s_wm1, 2)
            nc.vector.tensor_scalar(wexp[:, :].bitcast(I32), wmax[:, :].bitcast(I32), 0x7F800000, None, ALU.bitwise_and).then_inc(s_wm1, 1)
            dve.wait_ge(s_wm1, 3)
            nc.vector.reciprocal(fac[:, 4:7], wexp[:, :]).then_inc(s_wm1, 1)
            dve.wait_ge(s_wm1, 4)
            nc.vector.tensor_scalar(wscale[:, :], fac[:, 4:7], W_TOP, None, ALU.mult).then_inc(s_wm1, 1)
            nc.vector.tensor_scalar(fac[:, 0:1], wexp[:, 0:1], 1.0 / (W_TOP * X_SCALE), None, ALU.mult).then_inc(s_wm1, 1)
            nc.vector.tensor_scalar(fac[:, 1:2], fac[:, 4:5], 0.5 / (W_TOP * X_SCALE), None, ALU.mult).then_inc(s_wm1, 1)
            nc.vector.tensor_scalar(fac[:, 3:4], wexp[:, 0:1], wexp[:, 1:2], 2.0 / W_TOP, ALU.mult, ALU.mult).then_inc(s_wm1, 1)
            dve.wait_ge(s_wm1, 8)
            nc.vector.tensor_scalar(fac[:, 2:3], fac[:, 3:4], wexp[:, 2:3], None, ALU.mult).then_inc(s_fac, 1)

            def norm2(c):
                for t in range(4):
                    nc.vector.bn_stats(stats[:, t, :], x1[:, bass.ds(c * 4 + t, 1), :].rearrange("p a d -> p (a d)")).then_inc(s_st2, 1)
                dve.wait_ge(s_st2, c * 4 + 4)
                for t in range(4):
                    nc.vector.bn_aggr(mv[:, t, :], stats[:, t, :]).then_inc(s_mv2, 1)
                dve.wait_ge(s_mv2, c * 4 + 4)
                nc.vector.tensor_scalar(vare[:, bass.ds(c * 4, 4)], mv[:, 0:4, 1], EPS, None, ALU.add).then_inc(s_ve2, 1)
                dve.wait_ge(s_rstd2, c + 1)
                if c > 0:
                    dve.wait_ge(s_x2_ps, c)
                for t in range(4):
                    nc.vector.tensor_scalar(xn[:, t, :], x1[:, bass.ds(c * 4 + t, 1), :].rearrange("p a d -> p (a d)"),
                                            mv[:, t, 0:1], rstd[:, bass.ds(c * 4 + t, 1)], ALU.subtract, ALU.mult).then_inc(s_xn2, 1)
                dve.wait_ge(s_xh, c + 1)
                nc.vector.scalar_tensor_tensor(out=xl[:, bass.ds(c, 1), :], in0=ps[:, 5, :].unsqueeze(1), scalar=X_SCALE,
                                               in1=xh[:, bass.ds(c, 1), :], op0=ALU.mult, op1=ALU.subtract).then_inc(s_xl, 1)

            dve.wait_ge(s_x1, B)
            for c in range(NC):
                norm2(c)

            def hidden(i, u):
                dve.wait_ge(s_u, i + 1)
                dve.wait_ge(s_sg, i + 1)
                nc.vector.scalar_tensor_tensor(out=h32[u % 4][:, :], in0=ps[:, 2 + u % 2, :], scalar=fac[:, 1:2],
                                               in1=sg[u % 4][:, :], op0=ALU.mult, op1=ALU.mult).then_inc(s_h, 1)

            def low(i, u):
                dve.wait_ge(s_hh, i + 1)
                nc.vector.tensor_tensor(hl[u % 4][:, :], h32[u % 4][:, :], hh[u % 4][:, :], ALU.subtract).then_inc(s_hl, 1)

            def y_out(c, k):
                dve.wait_ge(s_d, c * (E * FT) + E * FT)
                if k != 0:
                    dve.wait_ge(s_y_ps, c)
                nc.vector.tensor_scalar(yT[:, :], ps[:, 4, :], fac[:, 2:3], None, ALU.mult).then_inc(s_yT, 1)

            def y_add(c, out_buf):
                dve.wait_ge(s_y_ps, c + 1)
                nc.vector.tensor_tensor(out_buf[:, :].rearrange("p (t d) -> p t d", d=D), ps[:, 6, :].rearrange("p (t d) -> p t d", d=D),
                                        x1[:, 4 * c:4 * c + 4, :], ALU.add).then_inc(s_y, 1)

            def body(e, first, chunk):
                for u in range(FT):
                    i = e * FT + u
                    hidden(i, u)
                    if not (first and u == 0):
                        low(i - 1, (u - 1) % 4)
                    if chunk is not None and u == 1:
                        y_out(chunk, chunk)
                if chunk is not None:
                    if chunk >= 2:
                        dve.wait_ge(s_out[chunk % 2], 16 * (chunk // 2))
                    y_add(chunk, y_sb[chunk % 2])

            body(0, True, None)
            with dve.Fori(1, E) as e:
                body(e, False, None)
            for c in range(1, NC):
                body(E * c, False, c - 1)
                with dve.Fori(E * c + 1, E * c + E) as e:
                    body(e, False, None)
            low(NC * E * FT - 1, 3)
            y_out(NC - 1, NC - 1)
            dve.wait_ge(s_out[(NC - 1) % 2], 16 * ((NC - 1) // 2))
            y_add(NC - 1, y_sb[(NC - 1) % 2])

        @block.tensor
        def _(pe):
            pe.wait_ge(s_ident, 1)
            pe.wait_ge(s_ctx, 16)
            for n in range(KT_TILES):
                mm = nc.tensor.transpose(ps[0:DC, 0, P * n:P * n + P], ctx_sb[:, n, :], ident[:, :])
            mm.then_inc(s_ctxT_ps, 1)
            pe.wait_ge(s_ctxT, 2)
            pe.wait_ge(s_vset, 4)
            pe.wait_ge(s_small, 16 * 6)
            nc.tensor.matmul(ps[:, 1, :], wk_sb[:, :], ctxT[:, :, 0, :], start=True, stop=True).then_inc(s_kv_ps, 1)
            for b in range(B):
                mm = nc.tensor.matmul(ps[:, 2 + b // 4, P * (b % 4):P * (b % 4) + P], ctxT[:, b, :, :].rearrange("p m k -> p (m k)"),
                                      wv_sb[:, :], start=True, stop=True)
            mm.then_inc(s_kv_ps, 1)
            for c in range(NC):
                pe.wait_ge(s_xn, 4 * c + 4)
                for t in range(4):
                    mm = nc.tensor.transpose(ps[:, 4 + c, P * t:P * t + P], xn[:, 4 * c + t, :], ident[:, :])
                mm.then_inc(s_xnT_ps, 1)
            pe.wait_ge(s_wq, 32)
            pe.wait_ge(s_xnT, NC)
            pe.wait_ge(s_v, 16)
            pe.wait_ge(s_kT, 1)
            pe.wait_ge(s_sel, 1)
            pe.wait_ge(s_ident, 2)

            def scores(b, i, reuse):
                g = 4 * i
                if reuse:
                    pe.wait_ge(s_x1, b - 1)
                nc.tensor.matmul(ps[:, g, 0:LQ], wq_sb[:, :], xnT[:, bass.ds(b * LQ, LQ)], start=True, stop=True).then_inc(s_q_ps, 1)
                pe.wait_ge(s_qT, b + 1)
                pe.wait_ge(s_kop, b + 1)
                for t in range(T):
                    for r in range(R):
                        rows = slice(32 * r, 32 * r + 32)
                        mm = nc.tensor.matmul(ps[:, g + r, J * LK * t:J * LK * (t + 1)], qT[i][rows, P * t:P * t + P],
                                              k_op[i][rows, :, :].rearrange("p j k -> p (j k)"), start=True, stop=True)
                mm.then_inc(s_s_ps, 1)

            def shifted(b, i):
                g = 4 * i
                pe.wait_ge(s_nml, b + 1)
                for t in range(T):
                    mm = nc.tensor.transpose(ps[:, g, 64 * t:64 * t + 64].bitcast(BF16),
                                             nmax_parts[i][:, t, :, :].rearrange("p r c -> p (r c)"), ident16[:, :])
                mm.then_inc(s_nmT_ps, 1)
                pe.wait_ge(s_nmT, b + 1)
                for t in range(2):
                    for part in range(2):
                        for r in range(R):
                            rows = slice(32 * r, 32 * r + 32)
                            dst = ps[:, g + r, LQ * t:LQ * t + LQ]
                            if part == 0:
                                mm = nc.tensor.matmul(dst, k_op[i][rows, 2 * t:2 * t + 2, :].rearrange("p j k -> p (j k)"),
                                                      qT[i][rows, :], start=True, stop=False)
                            else:
                                mm = nc.tensor.matmul(dst, max_sel[rows, 2 * t:2 * t + 2, :].rearrange("p j k -> p (j k)"),
                                                      nmaxT[i][rows, :], start=False, stop=True)
                mm.then_inc(s_st_ps, 1)

            def values(b, i):
                g = 4 * i
                pe.wait_ge(s_p, b * 2 + 2)
                for t in range(T):
                    for r in range(PAIRS):
                        c0 = (t * PAIRS + r) * VC
                        mm = nc.tensor.matmul(ps[:, g, c0:c0 + VC], prob[i][:, r, P * t:P * t + P],
                                              v_op[:, bass.ds(b, 1), r, :].rearrange("p a c -> p (a c)"), start=True, stop=True)
                mm.then_inc(s_o_ps, 1)

            def project(b, i):
                g = 4 * i
                pe.wait_ge(s_o, b * T + T)
                for t in range(T):
                    mm = nc.tensor.transpose(ps[:, g + 1, P * t:P * t + P], o_sb[i][:, t, :, :].rearrange("p h d -> p (h d)"), ident[:, :])
                mm.then_inc(s_oT_ps, 1)
                pe.wait_ge(s_oT, b + 1)
                for t in range(T):
                    mm = nc.tensor.matmul(ps[:, g + 2, D * t:D * t + D], oT[i][:, P * t:P * t + P], wo_sb[:, :], start=True, stop=True)
                mm.then_inc(s_wo_ps, 1)

            def step(b, i, reuse):
                scores(b, i, reuse)
                values(b - 1, 1 - i)
                shifted(b, i)
                project(b - 1, 1 - i)

            scores(0, 0, False)
            shifted(0, 0)
            step(1, 1, False)
            with pe.Fori(0, B // 2 - 1) as n:
                step(n * 2 + 2, 0, True)
                step(n * 2 + 3, 1, True)
            values(B - 1, 1)
            project(B - 1, 1)

            pe.wait_ge(s_x1, B)
            pe.wait_ge(s_wmax, 3)
            nc.tensor.transpose(ps[0:3, 7, 0:P], wmax[:, :], ident[:, :]).then_inc(s_wmT_ps, 1)
            pe.wait_ge(s_wd, 1)
            nc.tensor.matmul(ps[:, 6, 0:3], ones3[0:3, :], wmaxd[0:3, 0:3], start=True, stop=True).then_inc(s_wb_ps, 1)
            for c in range(NC):
                pe.wait_ge(s_xn2, c * 4 + 4)
                if c > 0:
                    pe.wait_ge(s_xl, c)
                for t in range(4):
                    mm = nc.tensor.transpose(ps[:, 5, P * t:P * t + P], xn[:, t, :], ident[:, :])
                mm.then_inc(s_x2_ps, 1)

            def three(dst, m, e, cols, hi, lo, start, stop):
                ws_hi = whi[m][:, bass.ds(e, 1), cols].rearrange("p a c -> p (a c)")
                ws_lo = wlo[m][:, bass.ds(e, 1), cols].rearrange("p a c -> p (a c)")
                nc.tensor.matmul(dst, ws_hi, hi, start=start, stop=False)
                nc.tensor.matmul(dst, ws_hi, lo, start=False, stop=False)
                return nc.tensor.matmul(dst, ws_lo, hi, start=False, stop=stop)

            def gate_up(i, c, e, u, fresh):
                if not fresh:
                    pe.wait_ge(s_sg, i - 1)
                cols = slice(P * u, P * u + P)
                hi, lo = (s[:, bass.ds(c, 1), :].rearrange("p a q -> p (a q)") for s in (xh, xl))
                three(ps[:, u % 2, :], 0, e, cols, hi, lo, True, True).then_inc(s_g, 1)
                if not fresh:
                    pe.wait_ge(s_h, i - 1)
                three(ps[:, 2 + u % 2, :], 1, e, cols, hi, lo, True, True).then_inc(s_u, 1)

            def down(i, e, u, start, stop):
                pe.wait_ge(s_hl, i + 1)
                three(ps[:, 4, :], 2, e, slice(P * u, P * u + P), hh[u][:, :], hl[u][:, :], start, stop).then_inc(s_d, 1)

            def body(c, e, first_of_all=False, first=False, arriving=False):
                if arriving:
                    pe.wait_ge(s_wl, e * 3 + 3)
                for u in range(FT):
                    i = (c * E + e) * FT + u
                    gate_up(i, c, e, u, first_of_all and u < 2)
                    if u < 2:
                        if not first_of_all:
                            prev = (E - 1) if first else e - 1
                            down(i - 2, prev, u + 2, False, first and u == 1)
                    else:
                        if first and u == 2 and not first_of_all:
                            pe.wait_ge(s_yT, c)
                        down(i - 2, e, u - 2, first and u == 2, False)

            def rows_back(c):
                pe.wait_ge(s_yT, c + 1)
                if type(c) is not int or c > 0:
                    pe.wait_ge(s_y, c)
                for t in range(4):
                    mm = nc.tensor.transpose(ps[:, 6, P * t:P * t + P], yT[:, P * t:P * t + P], ident[:, :])
                mm.then_inc(s_y_ps, 1)

            pe.wait_ge(s_xl, NC)
            body(0, 0, True, True, True)
            with pe.Fori(1, E) as e:
                body(0, e, arriving=True)
            with pe.Fori(1, NC) as c:
                body(c, 0, first=True)
                rows_back(c - 1)
                with pe.Fori(1, E) as e:
                    body(c, e)
            last = NC * E * FT
            down(last - 2, E - 1, 2, False, False)
            down(last - 1, E - 1, 3, False, True)
            rows_back(NC - 1)


_INS = ["x", "ctx_512", "L0_xattn_Wq", "L0_xattn_bq", "L0_xattn_Wk", "L0_xattn_bk", "L0_xattn_Wv", "L0_xattn_bv",
        "L0_xattn_Wo", "L0_xattn_bo", "L0_ffn_Wg", "L0_ffn_Wu", "L0_ffn_Wd"]


def kernel(**inputs):
    import numpy as np
    import concourse.bacc as bacc
    from concourse.bass_utils import run_bass_kernel_spmd

    nc = bacc.Bacc("TRN2", target_bir_lowering=False, num_devices=1)
    arrays, args = {}, []
    for name in _INS:
        a = np.ascontiguousarray(inputs[name])
        arrays[f"in_{name}"] = a
        args.append(nc.dram_tensor(f"in_{name}", a.shape, mybir.dt.from_np(a.dtype), kind="ExternalInput").ap())
    out = nc.dram_tensor("out_rows", inputs["x"].shape, F32, kind="ExternalOutput").ap()
    build(nc, *args, out)
    r = run_bass_kernel_spmd(nc, [arrays], core_ids=[0])
    return r.results[0]["out_rows"]
```

```python
from contextlib import ExitStack

import concourse.bass as bass
from concourse import mybir
from concourse.alu_op_type import AluOpType as ALU

F32 = mybir.dt.float32
BF16 = mybir.dt.bfloat16
F16 = mybir.dt.float16
I32 = mybir.dt.int32
F32R = mybir.dt.float32r
ACT = mybir.ActivationFunctionType
AX = mybir.AxisListType

P = 128
EPS = 1e-5
X_SCALE = 256.0
W_TOP = 2.0 ** 13


def build(nc, x, ctx_in, Wq, bq, Wk, bk, Wv, bv, Wo, bo, Wg, Wu, Wd, out):
    B, LQ, D = x.shape
    _, LK, DC = ctx_in.shape
    E, _, F = Wg.shape
    H = 16
    DH = D // H
    SCALE = float(DH) ** -0.5
    T = LQ // P
    NT = B * T
    R = 4
    J = H // R
    PAIRS = H // 2
    VC = 2 * DH + 2
    CB = 512 // LQ
    NC = B // CB
    CH = CB * LQ
    FT = F // P
    WE = FT * P
    KT_TILES = B * LK // P
    assert D == P and 2 * LK == P and FT == 4 and CH == 512 and NT == 16

    with ExitStack() as es:
        def sb(name, shape, dt=F32):
            return es.enter_context(nc.sbuf_tensor(name, shape, dt))

        def sem(name):
            return es.enter_context(nc.semaphore(name))

        x_sb = sb("x_sb", [P, NT, D])
        ctx_sb = sb("ctx_sb", [P, KT_TILES, DC])
        wq_sb = sb("wq_sb", [P, D])
        wk_sb = sb("wk_sb", [DC + 1, D])
        wv_sb = sb("wv_sb", [DC + 1, D])
        wo_sb = sb("wo_sb", [P, D])
        bq_sb = sb("bq_sb", [P, 1])
        bo_sb = sb("bo_sb", [P, D])
        w32 = sb("w32", [P, 3, E, WE])
        w16 = sb("w16", [P, 6, E, WE], F16)
        w_op = sb("w_op", [P, R, 3, 32])
        wk_op = sb("wk_op", [DC + 1, R, 3, 32])
        bq_op = sb("bq_op", [P, R])
        ident_op = sb("ident_op", [P, R, 3, 32])
        ident = sb("ident", [P, P])
        k_mask = sb("k_mask", [P, J])
        ones3 = sb("ones3", [3, P])
        half_c = sb("half_c", [P, 4])
        silu_c = sb("silu_c", [P, 4])
        bqs = sb("bqs", [P, 1])
        stats = sb("stats", [P, NT, 6])
        mv = sb("mv", [P, NT, 2])
        rstd = sb("rstd", [P, NT])
        vare = sb("vare", [P, NT])
        xn = sb("xn", [P, 8, D])
        xnT = [sb(f"xnT{i}", [P, CH]) for i in range(2)]
        xbo = x_sb
        x1 = x_sb
        xh = sb("xh", [P, NC, CH], F16)
        xl = sb("xl", [P, NC, CH], F16)
        ctxT = sb("ctxT", [DC + 1, B, 2, LK])
        q_hi = sb("q_hi", [P, B - CB, LQ], F32R)
        q_lo = sb("q_lo", [P, B - CB, LQ], F32R)
        q_all = w16[:, :, :, :].rearrange("p m e f -> p (m e f)").bitcast(F32R)[:, 0:R * (B - CB) * LQ].rearrange(
            "p (r b q) -> p r b q", r=R, b=B - CB)
        k_rows = sb("k_rows", [P, R, B, LK], F32R)
        v_res = sb("v_res", [P, B, PAIRS, DH])
        v_part = [sb(f"v_part{n}", [P, B, PAIRS, VC], BF16) for n in range(3)]
        q_op = sb("q_op", [P, 2, R, LQ], F32R)
        k_op = [sb(f"k_op{i}", [P, R, J * LK], F32R) for i in range(2)]
        nmax = [sb(f"nmax{i}", [P, 2, T, J]) for i in range(2)]
        nmax_parts = [sb(f"nmax_parts{i}", [P, 2, T, 32]) for i in range(2)]
        prob = [sb(f"prob{i}", [P, 4, LQ]) for i in range(2)]
        p_hi = [sb(f"p_hi{i}", [P, 4, LQ], F16) for i in range(2)]
        p_lo = [sb(f"p_lo{i}", [P, 4, LQ], F16) for i in range(2)]
        rsum = sb("rsum", [P, T, PAIRS, 2])
        o_sb = sb("o_sb", [P, T, H, DH])
        oT = sb("oT", [P, LQ])
        wmaxe = sb("wmaxe", [P, 3, E])
        wmax = sb("wmax", [P, 3])
        wmaxd = sb("wmaxd", [3, 4])
        wexp = sb("wexp", [P, 3])
        wscale = sb("wscale", [P, 3])
        fac = sb("fac", [P, 8])
        sg = [xnT[0][:, :], xnT[1][:, :]] + [sb(f"sg{i}", [P, CH])[:, :] for i in (2, 3)]
        h32 = [prob[i // 2][:, 2 * (i % 2):2 * (i % 2) + 2, :].rearrange("p r q -> p (r q)") for i in range(4)]
        hh = [p_hi[i // 2][:, 2 * (i % 2):2 * (i % 2) + 2, :].rearrange("p r q -> p (r q)") for i in range(4)]
        hl = [p_lo[i // 2][:, 2 * (i % 2):2 * (i % 2) + 2, :].rearrange("p r q -> p (r q)") for i in range(4)]
        yT = v_res[:, :, :, :].rearrange("p b r d -> p (b r d)")
        y_sb = [sb("y_sb", [P, CH])[:, :], xn[:, 4:8, :].rearrange("p t d -> p (t d)")]

        ps = es.enter_context(nc.psum_tensor("ps", [P, 8, 512], F32))
        s_table = sem("table_loaded")
        ST_BANK, O_BANK, OT_BANK = 4, 6, 7
        XT_BANK = (6, 4, 6, 4)
        Q_BANK = (4, 5, 7, 6, 5, 7, 5)
        X2_BANK = (1, 5, 5, 5)
        U = 2 * B

        s_x = [sem(f"x_loaded{c}") for c in range(NC)]
        s_bo, s_rep = sem("bo_loaded"), sem("weight_columns_repeated")
        s_wsc = sem("weights_scaled")
        s_wme = sem("expert_weight_max")
        s_qall = [sem(f"query_rows_loaded{c}") for c in range(1, NC)]
        s_ctx, s_wq, s_small = sem("ctx_loaded"), sem("wq_loaded"), sem("small_loaded")
        s_w = [sem(f"ffn_weights_loaded{n}") for n in range(E // 2)]
        s_ident, s_cst, s_pset, s_vset, s_mask = (sem("identity_set"), sem("constants_set"), sem("operands_cleared"), sem("ones_set"),
                                                  sem("mask_set"))
        s_bq_ps, s_bqr, s_wv, s_wo = sem("bq_in_psum"), sem("bq_loaded"), sem("wv_loaded"), sem("wo_loaded")
        s_ctxT_ps, s_ctxT, s_kT_ps, s_v_ps = sem("ctxT_in_psum"), sem("ctxT_copied"), sem("kT_in_psum"), sem("v_in_psum")
        s_kh, s_kl = sem("k_hi_ready"), sem("k_lo_ready")
        s_v1, s_vr, s_v2, s_v3 = sem("v_part1"), sem("v_residue"), sem("v_part2"), sem("v_part3")
        s_bqs = sem("query_scaled")
        s_st, s_mv, s_ve, s_rstd, s_xn = sem("ln1_stats"), sem("ln1_mean_var"), sem("ln1_var_eps"), sem("ln1_rstd"), sem("ln1_rows")
        s_xnT_ps, s_xnT, s_xbo = sem("xnT_in_psum"), sem("xnT_copied"), sem("x_plus_bo")
        s_q_ps, s_qh, s_ql = sem("q_in_psum"), sem("q_hi_ready"), sem("q_lo_ready")
        s_qop = [[sem(f"q_operand_loaded{i}_{h}") for h in range(2)] for i in range(2)]
        s_kop = sem("k_operand_ready")
        s_s_ps, s_nm, s_nmh, s_nml = sem("scores_in_psum"), sem("max_ready"), sem("max_hi"), sem("max_parts")
        s_nmT_ps, s_nmT = sem("maxT_in_psum"), sem("maxT_copied")
        s_st_ps, s_p, s_ph, s_pl = sem("shifted_in_psum"), sem("prob_ready"), sem("prob_hi"), sem("prob_lo")
        s_o_ps, s_rs, s_o = sem("out_in_psum"), sem("sums_inverted"), sem("out_normed")
        s_oT_ps, s_oT, s_wo_ps, s_x1 = sem("oT_in_psum"), sem("oT_copied"), sem("wo_in_psum"), sem("x1_ready")
        s_wmax, s_wmT_ps, s_wm1, s_wd = sem("weight_max"), sem("weight_maxT_in_psum"), sem("weight_max_all"), sem("weight_max_diag")
        s_wb_ps, s_fac = sem("weight_max_in_psum"), sem("factors")
        s_wh, s_wl = sem("weights_hi"), sem("weights_lo")
        s_st2, s_mv2, s_ve2, s_rstd2, s_xn2 = sem("ln2_stats"), sem("ln2_mean_var"), sem("ln2_var_eps"), sem("ln2_rstd"), sem("ln2_rows")
        s_x2_ps, s_xh, s_xl = sem("x2T_in_psum"), sem("x2T_hi"), sem("x2T_lo")
        s_g, s_u, s_sg, s_h, s_hh, s_hl, s_d = (sem("gate_in_psum"), sem("up_in_psum"), sem("silu_ready"), sem("h_ready"),
                                                sem("h_hi"), sem("h_lo"), sem("down_added"))
        s_yT, s_y_ps, s_y, s_out = sem("yT_ready"), sem("y_in_psum"), sem("y_ready"), [sem(f"rows_stored{i}") for i in range(2)]

        x_view = x.rearrange("b (p t) d -> p b t d", t=T)
        out_view = out.rearrange("b (p t) d -> p b t d", t=T)
        x_by_b = x_sb[:, :, :].rearrange("p (b t) d -> p b t d", t=T)
        c_view = ctx_in.rearrange("(n m) k d -> (m k) n d", n=KT_TILES)
        w_view = [Wg.rearrange("e p f -> p e f"), Wu.rearrange("e p f -> p e f"),
                  Wd.rearrange("e (t p) d -> p e t d", p=P)]

        block = es.enter_context(nc.Block())

        @block.sync
        def _(sp):
            def rows(c):
                sp.dma_start(x_by_b[:, CB * c:CB * c + CB], x_view[:, CB * c:CB * c + CB]).then_inc(s_x[c], 16)

            def weights(e):
                for m in range(3):
                    dst = w32[:, m, e:e + 2, :]
                    if m == 2:
                        dst = dst.rearrange("p e (t d) -> p e t d", t=FT)
                    sp.dma_start(dst, w_view[m][:, e:e + 2]).then_inc(s_w[e // 2], 16)

            sp.dma_start(ctx_sb[:, :, :], c_view).then_inc(s_ctx, 16)
            rows(0)
            sp.dma_start(wk_sb[0:DC, :], Wk).then_inc(s_small, 16)
            sp.dma_start(wk_sb[DC:DC + 1, :], bk.rearrange("(a d) -> a d", a=1)).then_inc(s_small, 16)
            sp.dma_start(bq_sb[:, :], bq.rearrange("(d a) -> d a", a=1)).then_inc(s_bqr, 16)
            sp.dma_start(wq_sb[:, :], Wq).then_inc(s_wq, 16)
            rows(1)
            sp.dma_start(wv_sb[0:DC, :], Wv).then_inc(s_wv, 16)
            sp.dma_start(wv_sb[DC:DC + 1, :], bv.rearrange("(a d) -> a d", a=1)).then_inc(s_wv, 16)
            rows(2)
            rows(3)
            for e in range(0, E, 2):
                weights(e)
            sp.dma_start(bo_sb[:, :], bo.partition_broadcast(P)).then_inc(s_bo, 16)
            sp.dma_start(wo_sb[:, :], Wo).then_inc(s_wo, 16)

            def query_rows(c):
                sp.wait_ge(s_qh, R + c)
                sp.wait_ge(s_ql, R + c)
                for r in range(R):
                    rows, b0 = slice(32 * r, 32 * r + 32), CB * (c - 1)
                    for n, src in enumerate((q_hi, q_lo)):
                        sp.dma_start(q_all[32 * n:32 * n + 32, r, b0:b0 + CB, :].bitcast(F32),
                                     src[rows, b0:b0 + CB, :].bitcast(F32)).then_inc(s_qall[c - 1], 16)

            def query_operand(b, i, h):
                sp.wait_ge(s_st_ps, b * 2 + (h - 3))
                for to, rows in ((slice(0, 64), slice(0, 64)), (slice(64, 96), slice(0, 32))):
                    sp.dma_start(q_op[to, i, 2 * h:2 * h + 2, :].bitcast(F32),
                                 q_all[rows, 2 * h:2 * h + 2, bass.ds(b - CB, 1), :].rearrange("p r a q -> p r (a q)").bitcast(F32)
                                 ).then_inc(s_qop[i][h], 16)

            def chunk_operands(b):
                for i in range(2):
                    for h in range(2):
                        query_operand(b + i, i, h)

            query_rows(1)
            query_rows(2)
            sp.wait_ge(s_qall[0], 16 * 2 * R)
            query_operand(2, 0, 0)
            query_operand(2, 0, 1)
            query_rows(3)
            query_operand(3, 1, 0)
            query_operand(3, 1, 1)
            for c in range(2, NC):
                sp.wait_ge(s_qall[c - 1], 16 * 2 * R)
            with sp.Fori(2, B // 2) as n:
                chunk_operands(n * 2)
            for c in range(NC):
                sp.wait_ge(s_y, c + 1)
                sp.dma_start(out_view[:, CB * c:CB * c + CB],
                             y_sb[c % 2].rearrange("p (b t d) -> p b t d", b=CB, t=T)).then_inc(s_out[c % 2], 16)
            for i in range(2):
                sp.wait_ge(s_out[i], 16 * NC // 2)

        @block.gpsimd
        def _(pool):
            pool.memset(ident[:, :], 0.0).then_inc(s_cst, 1)
            pool.wait_ge(s_cst, 1)
            pool.affine_select(out=ident[:, :], in_=ident[:, :], compare_op=ALU.not_equal, fill=1.0, base=0,
                               pattern=[[-1, P]], channel_multiplier=1).then_inc(s_ident, 1)
            pool.memset(half_c[:, :], -0.5).then_inc(s_cst, 1)
            pool.memset(k_rows[:, :, :, :].bitcast(F32), 1.0).then_inc(s_pset, 1)
            for n in range(3):
                pool.memset(v_part[n][:, :, :, :].rearrange("p b r c -> p (b r c)").bitcast(F32), 0.0).then_inc(s_pset, 1)
            for i in range(2):
                pool.memset(nmax_parts[i][:, :, :, :], 0.0).then_inc(s_pset, 1)
            pool.wait_ge(s_cst, 2)
            def root(c):
                pool.wait_ge(s_ve, c + 1)
                pool.tensor_tensor(rstd[:, 4 * c:4 * c + 4], vare[:, 4 * c:4 * c + 4], half_c[:, :], ALU.pow).then_inc(s_rstd, 1)

            def add_bo(c):
                pool.wait_ge(s_xn, 4 * c + 4)
                pool.tensor_tensor(xbo[:, 4 * c:4 * c + 4, :], x_sb[:, 4 * c:4 * c + 4, :],
                                   bo_sb[:, :].unsqueeze(1).to_broadcast([P, 4, D]), ALU.add).then_inc(s_xbo, 1)

            for c in range(NC):
                root(c)
            pool.wait_ge(s_bo, 16)
            for c in range(NC):
                add_bo(c)

            def prob_low(u, h, reuse):
                pool.wait_ge(s_ph, u + 1)
                if reuse:
                    pool.wait_ge(s_o_ps, u - 1)
                pool.tensor_tensor(p_lo[h][:, :, :], prob[h][:, :, :], p_hi[h][:, :, :], ALU.subtract).then_inc(s_pl, 1)

            def key_operand(u, b, i, h):
                pool.wait_ge(s_st_ps, u - 3)
                pool.tensor_tensor(k_op[i][:, 2 * h:2 * h + 2, :].rearrange("p r (j k) -> p r j k", j=J),
                                   k_rows[:, 2 * h:2 * h + 2, bass.ds(b, 1), :].bitcast(F32).to_broadcast([P, 2, J, LK]),
                                   k_mask[:, :].unsqueeze(1).unsqueeze(3).to_broadcast([P, 2, J, LK]), ALU.mult).then_inc(s_kop, 1)

            for u in range(4):
                prob_low(u, u % 2, u >= 2)
            pool.wait_ge(s_kop, 8)
            with pool.Fori(1, U // 4 - 1) as n:
                for v in range(4):
                    prob_low(n * 4 + v, v % 2, True)
                    key_operand(n * 4 + (v + 4), n * 2 + (v // 2 + 2), v // 2, v % 2)
            prob_low(U - 4, 0, True)

            def root2(c):
                pool.wait_ge(s_ve2, c + 1)
                pool.tensor_tensor(rstd[:, 4 * c:4 * c + 4], vare[:, 4 * c:4 * c + 4], half_c[:, :], ALU.pow).then_inc(s_rstd2, 1)

            def weights_low(e):
                for m in range(3):
                    pool.wait_ge(s_wh, e * 3 + (m + 1))
                    pool.tensor_tensor(w16[:, 3 + m, bass.ds(e, 1), :], w32[:, m, bass.ds(e, 1), :], w16[:, m, bass.ds(e, 1), :],
                                       ALU.subtract).then_inc(s_wl, 1)

            root2(0)
            for u in range(U - 3, U):
                prob_low(u, u % 2, True)
            weights_low(1)
            root2(1)
            with pool.Fori(2, E) as e:
                weights_low(e)
            for c in range(2, NC):
                root2(c)

        @block.scalar
        def _(act):
            act.wait_ge(s_cst, 2)
            nc.scalar.activation(silu_c[:, :], half_c[:, :], ACT.Exp).then_inc(s_table, 1)
            act.wait_ge(s_ctxT_ps, 1)
            for m in range(2):
                nc.scalar.copy(ctxT[0:DC, :, m, :], ps[0:DC, 7, :].rearrange("p (b k) -> p b k", k=LK)).then_inc(s_ctxT, 1)
            act.wait_ge(s_wq, 16)
            nc.scalar.mul(w_op[:, :, :, :], wq_sb[:, :].rearrange("p (r a d) -> p r a d", r=R, a=1).to_broadcast([P, R, 3, 32]), SCALE).then_inc(s_bqs, 1)
            act.wait_ge(s_bq_ps, 1)
            nc.scalar.mul(bq_op[0:3 * 32, :], ps[0:3 * 32, 4, 0:R], SCALE).then_inc(s_bqs, 1)

            def key_high(r):
                act.wait_ge(s_kT_ps, r + 1)
                if r == 0:
                    act.wait_ge(s_pset, 1)
                nc.scalar.copy(k_rows[0:3 * 32, r, :, :], ps[0:3 * 32, r, :].rearrange("p (b k) -> p b k", k=LK)).then_inc(s_kh, 1)

            def rows_T(c):
                act.wait_ge(s_xnT_ps, c + 1)
                nc.scalar.copy(xnT[c % 2][:, :], ps[:, XT_BANK[c], :]).then_inc(s_xnT, 1)

            def query_high(c):
                act.wait_ge(s_q_ps, R + c)
                nc.scalar.activation(q_hi[:, CB * (c - 1):CB * c, :], ps[:, Q_BANK[R + c - 1], :].rearrange("p (b q) -> p b q", q=LQ),
                                     ACT.Identity, bias=bqs[:, 0:1]).then_inc(s_qh, 1)

            def first_query_high(r):
                act.wait_ge(s_q_ps, r + 1)
                nc.scalar.activation(q_op[0:3 * 32, :, r, :], ps[0:3 * 32, Q_BANK[r], :].rearrange("p (b q) -> p b q", q=LQ),
                                     ACT.Identity, bias=bq_op[0:3 * 32, r:r + 1]).then_inc(s_qh, 1)

            key_high(0)
            key_high(1)
            rows_T(0)
            nc.scalar.mul(bqs[:, :], bq_sb[:, :], SCALE).then_inc(s_bqs, 1)
            act.wait_ge(s_bqs, 2)
            nc.scalar.mul(wq_sb[:, :], wq_sb[:, :], SCALE).then_inc(s_bqs, 1)
            key_high(2)
            key_high(3)
            act.wait_ge(s_bqs, 4)
            for r in range(R):
                first_query_high(r)
            rows_T(1)
            act.wait_ge(s_v_ps, 1)
            act.wait_ge(s_pset, 4)
            for n in range(2):
                for j in range(2):
                    half = slice(LK * j, LK * j + LK)
                    nc.scalar.copy(v_part[0][half, 4 * n:4 * n + 4, :, DH * j:DH * j + DH].rearrange("p b r d -> p (b r) d"),
                                   ps[half, 2 + n, :].rearrange("p (r j d) -> p r j d", j=2, d=DH)[:, :, j, :]).then_inc(s_v1, 1)
            query_high(1)
            rows_T(2)
            query_high(2)
            act.wait_ge(s_vr, 4)
            for j in range(2):
                half = slice(LK * j, LK * j + LK)
                nc.scalar.copy(v_part[1][half, :, :, DH * j:DH * j + DH].rearrange("p b r d -> p (b r) d"),
                               v_res[half, :, :, :].rearrange("p b r d -> p (b r) d")).then_inc(s_v2, 1)

            def shift_rows(u, i, h):
                act.wait_ge(s_nmT_ps, u + 1)
                nc.scalar.copy(q_op[3 * 32:P, i, 2 * h:2 * h + 2, :],
                               ps[0:32, 2 * h, :].rearrange("p (r q) -> p r q", r=2)).then_inc(s_nmT, 1)

            shift_rows(0, 0, 0)
            rows_T(3)
            query_high(3)

            def exps(u, h, reuse):
                act.wait_ge(s_st_ps, u + 1)
                if reuse:
                    act.wait_ge(s_pl, u - 1)
                nc.scalar.activation(prob[h][:, :, :], ps[:, ST_BANK:ST_BANK + 2, :].rearrange("p r (t q) -> p (r t) q", t=2),
                                     ACT.Exp).then_inc(s_p, 1)

            def high_part(u, h, reuse):
                act.wait_ge(s_p, u + 1)
                if reuse:
                    act.wait_ge(s_o_ps, u - 1)
                nc.scalar.copy(p_hi[h][:, :, :], prob[h][:, :, :]).then_inc(s_ph, 1)

            def out_T(b):
                act.wait_ge(s_oT_ps, b + 1)
                nc.scalar.copy(oT[:, :], ps[:, OT_BANK, 0:LQ]).then_inc(s_oT, 1)

            def slot(u, b, v, at):
                exps(u, v % 2, at >= 2)
                if at + 1 < U:
                    shift_rows(u + 1, (v + 1) // 2 % 2, (v + 1) % 2)
                if v % 2 == 0 and at >= 4:
                    out_T(b - 2)
                high_part(u, v % 2, at >= 2)

            def rows_high(c):
                act.wait_ge(s_x2_ps, c + 1)
                nc.scalar.activation(xh[:, c, :], ps[:, X2_BANK[c], :], ACT.Copy, scale=X_SCALE).then_inc(s_xh, 1)

            for u in range(4):
                slot(u, u // 2, u, u)
            with act.Fori(1, U // 4 - 1) as n:
                for v in range(4):
                    slot(n * 4 + v, n * 2 + v // 2, v, 4 + v)
            slot(U - 4, B - 2, 0, U - 4)
            slot(U - 3, B - 2, 1, U - 3)
            slot(U - 2, B - 1, 2, U - 2)
            rows_high(0)
            slot(U - 1, B - 1, 3, U - 1)
            act.wait_ge(s_table, 1)
            nc.scalar.activation(silu_c[:, :], half_c[:, :], ACT.Silu).then_inc(s_table, 1)
            out_T(B - 2)

            def weights(e):
                for m in range(3):
                    weight_high(m, e)

            def weight_high(m, e):
                act.wait_ge(s_wsc, e * 3 + (m + 1))
                nc.scalar.copy(w16[:, m, bass.ds(e, 1), :], w32[:, m, bass.ds(e, 1), :]).then_inc(s_wh, 1)

            weights(0)

            def silu(i, u):
                act.wait_ge(s_g, i + 1)
                nc.scalar.activation(sg[u], ps[:, u % 2, :], ACT.Silu, scale=fac[:, 0:1]).then_inc(s_sg, 1)

            def high(i, u):
                act.wait_ge(s_h, i + 1)
                nc.scalar.copy(hh[u], h32[u]).then_inc(s_hh, 1)

            def body(e, fresh, split=False):
                for u in range(FT):
                    i = e * FT + u
                    if not fresh:
                        act.wait_ge(s_h, i - 3)
                    silu(i, u)
                    if not (fresh and u == 0):
                        if not fresh:
                            act.wait_ge(s_d, i - 4)
                        high(i - 1, (u - 1) % 4)
                    if split and u < 3:
                        weight_high(u, e + 1)

            body(0, True, True)
            out_T(B - 1)
            rows_high(1)
            with act.Fori(1, E - 1) as e:
                body(e, False, True)
            body(E - 1, False)
            for c in range(1, NC):
                body(E * c, False)
                if c + 1 < NC:
                    rows_high(c + 1)
                with act.Fori(E * c + 1, E * c + E) as e:
                    body(e, False)
            act.wait_ge(s_d, NC * E * FT - 4)
            high(NC * E * FT - 1, 3)

        @block.vector
        def _(dve):
            nc.vector.memset(ctxT[DC:DC + 1, :, :, :], 1.0).then_inc(s_vset, 1)
            nc.vector.memset(ones3[:, :], 1.0).then_inc(s_vset, 1)
            dve.wait_ge(s_ident, 1)
            nc.vector.tensor_copy(ident_op[:, :, :, :], ident[:, :].rearrange("p (r a d) -> p r a d", r=R, a=1).to_broadcast([P, R, 3, 32])).then_inc(s_rep, 1)
            nc.vector.tensor_reduce(k_mask[0:3 * 32, :], ident[0:3 * 32, :].rearrange("p (a j d) -> p j a d", j=J, d=DH), AX.XY, ALU.add).then_inc(s_mask, 1)
            nc.vector.tensor_reduce(k_mask[3 * 32:P, :], ident[3 * 32:P, :].rearrange("p (n c) -> p c n", c=J), AX.X, ALU.add).then_inc(s_mask, 1)
            def norm_stats(c):
                dve.wait_ge(s_x[c], 16)
                for t in range(4 * c, 4 * c + 4):
                    nc.vector.bn_stats(stats[:, t, :], x_sb[:, t, :]).then_inc(s_st, 1)
                for t in range(4 * c, 4 * c + 4):
                    dve.wait_ge(s_st, t + 1)
                    nc.vector.bn_aggr(mv[:, t, :], stats[:, t, :]).then_inc(s_mv, 1)
                dve.wait_ge(s_mv, 4 * c + 4)
                nc.vector.tensor_scalar(vare[:, 4 * c:4 * c + 4], mv[:, 4 * c:4 * c + 4, 1], EPS, None, ALU.add).then_inc(s_ve, 1)

            def norm_rows(c):
                dve.wait_ge(s_rstd, c + 1)
                if c >= 2:
                    dve.wait_ge(s_xnT_ps, c - 1)
                for t in range(4 * c, 4 * c + 4):
                    nc.vector.tensor_scalar(xn[:, t % 8, :], x_sb[:, t, :], mv[:, t, 0:1], rstd[:, t:t + 1], ALU.subtract, ALU.mult).then_inc(s_xn, 1)

            def key_low(r):
                dve.wait_ge(s_kh, r + 1)
                nc.vector.tensor_tensor(k_rows[64:96, r, :, :], ps[64:96, r, :].rearrange("p (b k) -> p b k", k=LK),
                                        k_rows[64:96, r, :, :].bitcast(F32), ALU.subtract).then_inc(s_kl, 1)

            def first_query_low(r):
                dve.wait_ge(s_qh, r + 1)
                nc.vector.scalar_tensor_tensor(out=q_op[32:64, :, r, :], in0=ps[32:64, Q_BANK[r], :].rearrange("p (b q) -> p b q", q=LQ),
                                               scalar=bq_op[32:64, r:r + 1], in1=q_op[32:64, :, r, :].bitcast(F32),
                                               op0=ALU.add, op1=ALU.subtract).then_inc(s_ql, 1)

            def query_low(c):
                dve.wait_ge(s_qh, R + c)
                nc.vector.scalar_tensor_tensor(out=q_lo[:, CB * (c - 1):CB * c, :], in0=ps[:, Q_BANK[R + c - 1], :].rearrange("p (b q) -> p b q", q=LQ),
                                               scalar=bqs[:, 0:1], in1=q_hi[:, CB * (c - 1):CB * c, :].bitcast(F32),
                                               op0=ALU.add, op1=ALU.subtract).then_inc(s_ql, 1)

            def key_operand(u, b, i, h, reuse):
                if reuse:
                    dve.wait_ge(s_st_ps, u - 3)
                nc.vector.tensor_tensor(k_op[i][:, 2 * h:2 * h + 2, :].rearrange("p r (j k) -> p r j k", j=J),
                                        k_rows[:, 2 * h:2 * h + 2, bass.ds(b, 1), :].bitcast(F32).to_broadcast([P, 2, J, LK]),
                                        k_mask[:, :].unsqueeze(1).unsqueeze(3).to_broadcast([P, 2, J, LK]), ALU.mult).then_inc(s_kop, 1)

            def value_residue():
                dve.wait_ge(s_v1, 4)
                for n in range(2):
                    for j in range(2):
                        half = slice(LK * j, LK * j + LK)
                        nc.vector.tensor_tensor(v_res[half, 4 * n:4 * n + 4, :, :].rearrange("p b r d -> p (b r) d"),
                                                ps[half, 2 + n, :].rearrange("p (r j d) -> p r j d", j=2, d=DH)[:, :, j, :],
                                                v_part[0][half, 4 * n:4 * n + 4, :, DH * j:DH * j + DH].rearrange("p b r d -> p (b r) d"),
                                                ALU.subtract).then_inc(s_vr, 1)

            def value_last():
                dve.wait_ge(s_v2, 2)
                for j in range(2):
                    half = slice(LK * j, LK * j + LK)
                    nc.vector.tensor_tensor(v_part[2][half, :, :, DH * j:DH * j + DH].rearrange("p b r d -> p (b r) d"),
                                            v_res[half, :, :, :].rearrange("p b r d -> p (b r) d"),
                                            v_part[1][half, :, :, DH * j:DH * j + DH].rearrange("p b r d -> p (b r) d"),
                                            ALU.subtract).then_inc(s_v3, 1)

            def row_max(u, h):
                dve.wait_ge(s_s_ps, u + 1)
                nc.vector.tensor_reduce(nmax[h][:, :, :, :], ps[:, 2 * h:2 * h + 2, :].rearrange("p r (t j k) -> p (r t j) k", t=T, j=J),
                                        AX.X, ALU.max, negate=True).then_inc(s_nm, 1)
                dve.wait_ge(s_nm, u + 1)
                hi, lo = nmax_parts[h][:, :, :, 0:J], nmax_parts[h][:, :, :, J:2 * J]
                nc.vector.tensor_copy(hi.bitcast(F32R), nmax[h][:, :, :, :]).then_inc(s_nmh, 1)
                dve.wait_ge(s_nmh, u + 1)
                nc.vector.tensor_tensor(lo, nmax[h][:, :, :, :], hi, ALU.subtract).then_inc(s_nml, 1)

            def norm_out(b):
                dve.wait_ge(s_o_ps, b * 2 + 2)
                o_ps = ps[:, O_BANK, 0:T * PAIRS * VC].rearrange("p (t r c) -> p t r c", t=T, c=VC)
                nc.vector.reciprocal(rsum[:, :, :, :], o_ps[:, :, :, 2 * DH:VC]).then_inc(s_rs, 1)
                dve.wait_ge(s_rs, b + 1)
                for t in range(T):
                    nc.vector.tensor_tensor(o_sb[:, t, :, :].rearrange("p (r j) d -> p r j d", j=2),
                                            o_ps[:, t, :, 0:2 * DH].rearrange("p r (j d) -> p r j d", j=2),
                                            rsum[:, t, :, :].unsqueeze(3).to_broadcast([P, PAIRS, 2, DH]), ALU.mult).then_inc(s_o, 1)

            def residual(b):
                dve.wait_ge(s_wo_ps, b + 1)
                nc.vector.tensor_tensor(x1[:, bass.ds(b * T, T), :], ps[:, OT_BANK, LQ:2 * LQ].rearrange("p (t d) -> p t d", t=T),
                                        xbo[:, bass.ds(b * T, T), :], ALU.add).then_inc(s_x1, 1)

            def weight_scale(m, e):
                nc.vector.tensor_scalar(w32[:, m, bass.ds(e, 1), :], w32[:, m, bass.ds(e, 1), :], wscale[:, m:m + 1], None, ALU.mult).then_inc(s_wsc, 1)

            def weights_low0():
                for m in range(3):
                    dve.wait_ge(s_wh, m + 1)
                    nc.vector.tensor_tensor(w16[:, 3 + m, 0, :], w32[:, m, 0, :], w16[:, m, 0, :], ALU.subtract).then_inc(s_wl, 1)

            def norm2(c):
                dve.wait_ge(s_x1, CB * (c + 1))
                for t in range(4):
                    nc.vector.bn_stats(stats[:, t, :], x1[:, c * 4 + t, :]).then_inc(s_st2, 1)
                dve.wait_ge(s_st2, c * 4 + 4)
                for t in range(4):
                    nc.vector.bn_aggr(mv[:, t, :], stats[:, t, :]).then_inc(s_mv2, 1)
                dve.wait_ge(s_mv2, c * 4 + 4)
                nc.vector.tensor_scalar(vare[:, 4 * c:4 * c + 4], mv[:, 0:4, 1], EPS, None, ALU.add).then_inc(s_ve2, 1)
                if c > 0:
                    dve.wait_ge(s_x2_ps, c)

            def norm2_rows(c):
                dve.wait_ge(s_rstd2, c + 1)
                for t in range(4):
                    nc.vector.tensor_scalar(xn[:, t, :], x1[:, c * 4 + t, :], mv[:, t, 0:1], rstd[:, c * 4 + t:c * 4 + t + 1],
                                            ALU.subtract, ALU.mult).then_inc(s_xn2, 1)

            def rows_low(c):
                dve.wait_ge(s_xh, c + 1)
                nc.vector.scalar_tensor_tensor(out=xl[:, c, :], in0=ps[:, X2_BANK[c], :], scalar=X_SCALE,
                                               in1=xh[:, c, :], op0=ALU.mult, op1=ALU.subtract).then_inc(s_xl, 1)

            def weights_max(e):
                nc.vector.tensor_reduce(wmaxe[:, :, bass.ds(e, 1)], w32[:, :, bass.ds(e, 1), :], AX.X, ALU.max,
                                        apply_absolute_value=True).then_inc(s_wme, 1)

            def slot(u, b, v, at):
                if v % 2 == 1 and at >= 5:
                    residual(b - 2)
                if v % 2 == 1 and at >= 3:
                    norm_out(b - 1)
                if at + 2 < U:
                    row_max(u + 2, v % 2)
                if at < 4:
                    key_operand(u + 4, b + 2, v // 2, v % 2, True)

            norm_stats(0)
            dve.wait_ge(s_small, 32)
            nc.vector.tensor_copy(wk_op[:, :, :, :], wk_sb[:, :].rearrange("p (r a d) -> p r a d", r=R, a=1).to_broadcast([DC + 1, R, 3, 32])).then_inc(s_rep, 1)
            dve.wait_ge(s_pset, 4)
            for j in range(2):
                nc.vector.memset(v_part[0][LK * j:LK * j + LK, :, :, 2 * DH + j], 1.0).then_inc(s_vset, 1)
            norm_rows(0)
            key_low(0)
            norm_stats(1)
            key_low(1)
            norm_stats(2)
            key_low(2)
            norm_rows(1)
            key_low(3)
            dve.wait_ge(s_mask, 2)
            dve.wait_ge(s_kl, R)
            key_operand(0, 0, 0, 0, False)
            norm_stats(3)
            first_query_low(0)
            first_query_low(1)
            key_operand(1, 0, 0, 1, False)
            first_query_low(2)
            first_query_low(3)
            norm_rows(2)
            dve.wait_ge(s_pset, 6)
            row_max(0, 0)
            norm_rows(3)
            value_residue()
            query_low(1)
            row_max(1, 1)
            query_low(2)
            value_last()
            query_low(3)
            key_operand(2, 1, 1, 0, False)
            key_operand(3, 1, 1, 1, False)
            for n in range(E // 2):
                dve.wait_ge(s_w[n], 48)
            for u in range(4):
                slot(u, u // 2, u, u)
                if u % 2 == 1:
                    weights_max(u // 2)
            dve.wait_ge(s_xbo, NC)
            with dve.Fori(1, U // 4 - 1) as n:
                for v in range(4):
                    slot(n * 4 + v, n * 2 + v // 2, v, 4 + v)
                    if v % 2 == 0:
                        weights_max(n * 2 + v // 2)
            slot(U - 4, B - 2, 0, U - 4)
            norm2(0)
            weights_max(E - 2)
            slot(U - 3, B - 2, 1, U - 3)
            weights_max(E - 1)
            dve.wait_ge(s_wme, E)
            nc.vector.tensor_reduce(wmax[:, :], wmaxe[:, :, :], AX.X, ALU.max).then_inc(s_wmax, 1)
            norm2_rows(0)
            dve.wait_ge(s_wmT_ps, 1)
            nc.vector.tensor_reduce(wmaxd[:, 3:4], ps[0:3, 0, 0:P], AX.X, ALU.max).then_inc(s_wm1, 1)
            dve.wait_ge(s_wm1, 1)
            nc.vector.tensor_scalar(wmaxd[:, 0:3], ident[0:3, 0:3], wmaxd[:, 3:4], None, ALU.mult).then_inc(s_wd, 1)
            dve.wait_ge(s_wb_ps, 1)
            nc.vector.tensor_scalar(wmax[:, :], ps[:, 0, LQ:LQ + 3], 1e-30, 1e30, ALU.max, ALU.min).then_inc(s_wm1, 1)
            dve.wait_ge(s_wm1, 2)
            nc.vector.tensor_scalar(wexp[:, :].bitcast(I32), wmax[:, :].bitcast(I32), 0x7F800000, None, ALU.bitwise_and).then_inc(s_wm1, 1)
            dve.wait_ge(s_wm1, 3)
            nc.vector.reciprocal(fac[:, 4:7], wexp[:, :]).then_inc(s_wm1, 1)
            dve.wait_ge(s_wm1, 4)
            nc.vector.tensor_scalar(wscale[:, :], fac[:, 4:7], W_TOP, None, ALU.mult).then_inc(s_wm1, 1)
            nc.vector.tensor_scalar(fac[:, 0:1], wexp[:, 0:1], 1.0 / (W_TOP * X_SCALE), None, ALU.mult).then_inc(s_wm1, 1)
            nc.vector.tensor_scalar(fac[:, 1:2], fac[:, 4:5], 0.5 / (W_TOP * X_SCALE), None, ALU.mult).then_inc(s_wm1, 1)
            nc.vector.tensor_scalar(fac[:, 3:4], wexp[:, 0:1], wexp[:, 1:2], 2.0 / W_TOP, ALU.mult, ALU.mult).then_inc(s_wm1, 1)
            dve.wait_ge(s_wm1, 8)
            nc.vector.tensor_scalar(fac[:, 2:3], fac[:, 3:4], wexp[:, 2:3], None, ALU.mult).then_inc(s_fac, 1)

            dve.wait_ge(s_fac, 1)
            for m in range(3):
                weight_scale(m, 0)
            slot(U - 1, B - 1, 3, U - 1)
            rows_low(0)
            weights_low0()
            residual(B - 2)
            norm_out(B - 1)

            def hidden(i, u):
                dve.wait_ge(s_u, i + 1)
                dve.wait_ge(s_sg, i + 1)
                nc.vector.scalar_tensor_tensor(out=h32[u], in0=ps[:, 2 + u % 2, :], scalar=fac[:, 1:2],
                                               in1=sg[u], op0=ALU.mult, op1=ALU.mult).then_inc(s_h, 1)

            def low(i, u):
                dve.wait_ge(s_hh, i + 1)
                nc.vector.tensor_tensor(hl[u], h32[u], hh[u], ALU.subtract).then_inc(s_hl, 1)

            def y_out(c):
                dve.wait_ge(s_d, (c + 1) * (E * FT))
                if c > 0:
                    dve.wait_ge(s_y_ps, c)
                nc.vector.tensor_scalar(yT, ps[:, 4, :], fac[:, 2:3], None, ALU.mult).then_inc(s_yT, 1)

            def y_add(c):
                dve.wait_ge(s_y_ps, c + 1)
                if c >= 2:
                    dve.wait_ge(s_out[c % 2], 16 * (c // 2))
                nc.vector.tensor_tensor(y_sb[c % 2].rearrange("p (t d) -> p t d", d=D), ps[:, 6, :].rearrange("p (t d) -> p t d", d=D),
                                        x1[:, 4 * c:4 * c + 4, :], ALU.add).then_inc(s_y, 1)

            def body(e, fresh=False, c=None, split=False):
                for u in range(FT):
                    i = e * FT + u
                    if split and u < 3:
                        weight_scale(u, e + 1)
                    hidden(i, u)
                    if not (fresh and u == 0):
                        low(i - 1, (u - 1) % 4)
                    if c is not None:
                        if u == 1 and c > 0:
                            y_out(c - 1)
                        if u == 1 and c + 1 < NC:
                            norm2(c + 1)
                        if u == 2 and c + 1 < NC:
                            norm2_rows(c + 1)
                if c is not None:
                    if c > 0:
                        y_add(c - 1)
                    if c + 1 < NC:
                        rows_low(c + 1)

            body(0, True, 0, True)
            residual(B - 1)
            with dve.Fori(1, E - 1) as e:
                body(e, split=True)
            body(E - 1)
            for c in range(1, NC):
                body(E * c, False, c)
                with dve.Fori(E * c + 1, E * c + E) as e:
                    body(e)
            low(NC * E * FT - 1, 3)
            y_out(NC - 1)
            y_add(NC - 1)

        @block.tensor
        def _(pe):
            pe.wait_ge(s_ident, 1)
            def warm(count):
                for _ in range(count):
                    nc.tensor.transpose(ps[:, 5, 0:P], ident[:, :], ident[:, :])

            warm(12)
            pe.wait_ge(s_ctx, 16)
            for n in range(KT_TILES):
                mm = nc.tensor.transpose(ps[0:DC, 7, P * n:P * n + P], ctx_sb[:, n, :], ident[:, :])
            mm.then_inc(s_ctxT_ps, 1)

            pe.wait_ge(s_rep, 2)
            pe.wait_ge(s_bqr, 16)
            for r in range(R):
                mm = nc.tensor.matmul(ps[0:3 * 32, 4, r:r + 1], ident_op[:, r, :, :].rearrange("p a d -> p (a d)"), bq_sb[:, :], start=True, stop=True)
            mm.then_inc(s_bq_ps, 1)
            warm(10)

            def keys(r):
                nc.tensor.matmul(ps[0:3 * 32, r, :], wk_op[:, r, :, :].rearrange("p a d -> p (a d)"), ctxT[:, :, 0, :], start=True, stop=True).then_inc(s_kT_ps, 1)

            def rows_T(c):
                pe.wait_ge(s_xn, 4 * c + 4)
                for t in range(4):
                    mm = nc.tensor.transpose(ps[:, XT_BANK[c], P * t:P * t + P], xn[:, (4 * c + t) % 8, :], ident[:, :])
                mm.then_inc(s_xnT_ps, 1)

            def first_queries(r):
                nc.tensor.matmul(ps[0:3 * 32, Q_BANK[r], :], w_op[:, r, :, :].rearrange("p a d -> p (a d)"), xnT[0][:, :], start=True, stop=True).then_inc(s_q_ps, 1)

            def queries(c):
                pe.wait_ge(s_xnT, c + 1)
                nc.tensor.matmul(ps[:, Q_BANK[R + c - 1], :], wq_sb[:, :], xnT[c % 2][:, :], start=True, stop=True).then_inc(s_q_ps, 1)

            def scores(u, i, h, reuse):
                pe.wait_ge(s_kop, u + 1)
                if reuse:
                    pe.wait_ge(s_nmT, u - 1)
                for t in range(T):
                    for r in range(2):
                        mm = nc.tensor.matmul(ps[:, 2 * h + r, J * LK * t:J * LK * (t + 1)], q_op[0:3 * 32, i, 2 * h + r, P * t:P * t + P],
                                              k_op[i][0:3 * 32, 2 * h + r, :], start=True, stop=True)
                mm.then_inc(s_s_ps, 1)

            def maxima_T(u, h):
                pe.wait_ge(s_nml, u + 1)
                for r in range(2):
                    for t in range(T):
                        mm = nc.tensor.transpose(ps[0:32, 2 * h, LQ * r + P * t:LQ * r + P * t + P], nmax_parts[h][:, r, t, :], ident[:, :])
                mm.then_inc(s_nmT_ps, 1)

            def shifted(u, i, h, reuse):
                pe.wait_ge(s_nmT, u + 1)
                if reuse:
                    pe.wait_ge(s_p, u)
                for r in range(2):
                    for t in range(2):
                        mm = nc.tensor.matmul(ps[:, ST_BANK + r, LQ * t:LQ * t + LQ], k_op[i][:, 2 * h + r, P * t:P * t + P],
                                              q_op[:, i, 2 * h + r, :], start=True, stop=True)
                mm.then_inc(s_st_ps, 1)

            def values(u, b, h, reuse):
                pe.wait_ge(s_ph, u + 1)
                pe.wait_ge(s_pl, u + 1)
                if reuse and h == 0:
                    pe.wait_ge(s_o, b * T)
                for t in range(T):
                    for r in range(4):
                        c0 = (t * PAIRS + 4 * h + r) * VC
                        terms = [(p_hi, 0), (p_hi, 1), (p_hi, 2), (p_lo, 0), (p_lo, 1), (p_lo, 2)]
                        for k, (part, n) in enumerate(terms):
                            mm = nc.tensor.matmul(ps[:, O_BANK, c0:c0 + VC], part[h][:, r, P * t:P * t + P],
                                                  v_part[n][:, bass.ds(b, 1), 4 * h + r, :].rearrange("p a c -> p (a c)"),
                                                  start=(k == 0), stop=(k == len(terms) - 1))
                mm.then_inc(s_o_ps, 1)

            def out_T(b):
                pe.wait_ge(s_o, b * T + T)
                for t in range(T):
                    mm = nc.tensor.transpose(ps[:, OT_BANK, P * t:P * t + P], o_sb[:, t, :, :].rearrange("p h d -> p (h d)"), ident[:, :])
                mm.then_inc(s_oT_ps, 1)

            def project(b):
                pe.wait_ge(s_oT, b + 1)
                for t in range(T):
                    mm = nc.tensor.matmul(ps[:, OT_BANK, LQ + D * t:LQ + D * t + D], oT[:, P * t:P * t + P], wo_sb[:, :], start=True, stop=True)
                mm.then_inc(s_wo_ps, 1)

            def rows2_T(c):
                pe.wait_ge(s_xn2, c * 4 + 4)
                for t in range(4):
                    mm = nc.tensor.transpose(ps[:, X2_BANK[c], P * t:P * t + P], xn[:, t, :], ident[:, :])
                mm.then_inc(s_x2_ps, 1)

            def slot(u, b, v, at, n):
                i, h = v // 2, v % 2
                if at + 2 < U:
                    if at >= 2:
                        pe.wait_ge(s_qop[1 - i][h], n * 32 + 32 * i)
                    scores(u + 2, 1 - i, h, True)
                if at + 1 < U:
                    shifted(u + 1, (v + 1) // 2 % 2, (v + 1) % 2, True)
                if h == 0 and at >= 4:
                    project(b - 2)
                if at >= 1:
                    values(u - 1, b - 1 + h, 1 - h, h == 1 and at >= 3)
                if at + 2 < U:
                    maxima_T(u + 2, h)
                if h == 1 and at >= 3:
                    out_T(b - 1)

            pe.wait_ge(s_ctxT, 2)
            pe.wait_ge(s_vset, 1)
            keys(0)
            keys(1)
            rows_T(0)
            keys(2)
            keys(3)
            pe.wait_ge(s_xnT, 1)
            pe.wait_ge(s_bqs, 2)
            for r in range(R):
                first_queries(r)
            pe.wait_ge(s_ql, 1)
            rows_T(1)
            pe.wait_ge(s_ql, 2)
            pe.wait_ge(s_bqs, 4)
            queries(1)
            scores(0, 0, 0, False)
            pe.wait_ge(s_kl, R)
            pe.wait_ge(s_wv, 32)
            for b in range(B):
                mm = nc.tensor.matmul(ps[:, 2 + b // 4, P * (b % 4):P * (b % 4) + P], ctxT[:, b, :, :].rearrange("p m k -> p (m k)"),
                                      wv_sb[:, :], start=True, stop=True)
            mm.then_inc(s_v_ps, 1)
            pe.wait_ge(s_ql, R)
            rows_T(2)
            queries(2)
            pe.wait_ge(s_vr, 4)
            scores(1, 0, 1, False)
            maxima_T(0, 0)
            rows_T(3)
            pe.wait_ge(s_ql, R + 1)
            queries(3)
            pe.wait_ge(s_ql, R + NC - 1)
            shifted(0, 0, 0, False)
            maxima_T(1, 1)
            pe.wait_ge(s_v3, 2)
            pe.wait_ge(s_wo, 16)
            for u in range(4):
                slot(u, u // 2, u, u, 0)
            with pe.Fori(1, U // 4 - 1) as n:
                for v in range(4):
                    slot(n * 4 + v, n * 2 + v // 2, v, 4 + v, n)
            slot(U - 4, B - 2, 0, U - 4, U // 4 - 1)
            slot(U - 3, B - 2, 1, U - 3, U // 4 - 1)
            pe.wait_ge(s_wmax, 1)
            nc.tensor.transpose(ps[0:3, 0, 0:P], wmax[:, :], ident[:, :]).then_inc(s_wmT_ps, 1)
            rows2_T(0)
            slot(U - 2, B - 1, 2, U - 2, U // 4 - 1)
            pe.wait_ge(s_wd, 1)
            nc.tensor.matmul(ps[:, 0, LQ:LQ + 3], ones3[0:3, :], wmaxd[0:3, 0:3], start=True, stop=True).then_inc(s_wb_ps, 1)
            slot(U - 1, B - 1, 3, U - 1, U // 4 - 1)
            project(B - 2)
            values(U - 1, B - 1, 1, False)

            def three(dst, m, e, cols, hi, lo, start, stop):
                ws_hi = w16[:, m, bass.ds(e, 1), cols].rearrange("p a c -> p (a c)")
                ws_lo = w16[:, 3 + m, bass.ds(e, 1), cols].rearrange("p a c -> p (a c)")
                nc.tensor.matmul(dst, ws_hi, hi, start=start, stop=False)
                nc.tensor.matmul(dst, ws_hi, lo, start=False, stop=False)
                return nc.tensor.matmul(dst, ws_lo, hi, start=False, stop=stop)

            def gate_up(i, c, e, u, fresh, arriving):
                if arriving:
                    pe.wait_ge(s_wl, e * 3 + 1)
                if not fresh:
                    pe.wait_ge(s_sg, i - 1)
                cols = slice(P * u, P * u + P)
                three(ps[:, u % 2, :], 0, e, cols, xh[:, c, :], xl[:, c, :], True, True).then_inc(s_g, 1)
                if arriving:
                    pe.wait_ge(s_wl, e * 3 + 2)
                if not fresh:
                    pe.wait_ge(s_h, i - 1)
                three(ps[:, 2 + u % 2, :], 1, e, cols, xh[:, c, :], xl[:, c, :], True, True).then_inc(s_u, 1)

            def down(i, e, u, start, stop):
                pe.wait_ge(s_hl, i + 1)
                three(ps[:, 4, :], 2, e, slice(P * u, P * u + P), hh[u], hl[u], start, stop).then_inc(s_d, 1)

            def body(c, e, first=False, arriving=False):
                fresh = c == 0 and first
                for u in range(FT):
                    i = (c * E + e) * FT + u
                    gate_up(i, c, e, u, fresh and u < 2, arriving and u == 0)
                    if u < 2:
                        if not fresh:
                            down(i - 2, (E - 1) if first else e - 1, u + 2, False, first and u == 1)
                    else:
                        if first and u == 2 and c > 0:
                            pe.wait_ge(s_yT, c)
                        if arriving and u == 2:
                            pe.wait_ge(s_wl, e * 3 + 3)
                        down(i - 2, e, u - 2, first and u == 2, False)

            def rows_back(c):
                pe.wait_ge(s_yT, c + 1)
                if c > 0:
                    pe.wait_ge(s_y, c)
                for t in range(4):
                    mm = nc.tensor.transpose(ps[:, 6, P * t:P * t + P], yT[:, P * t:P * t + P], ident[:, :])
                mm.then_inc(s_y_ps, 1)

            pe.wait_ge(s_xl, 1)
            for c in range(NC):
                if c > 0:
                    pe.wait_ge(s_xl, c + 1)
                body(c, 0, first=True, arriving=(c == 0))
                if c == 0:
                    out_T(B - 1)
                    project(B - 1)
                if c > 0:
                    rows_back(c - 1)
                if c + 1 < NC:
                    rows2_T(c + 1)
                with pe.Fori(1, E) as e:
                    body(c, e, arriving=(c == 0))
            last = NC * E * FT
            down(last - 2, E - 1, 2, False, False)
            down(last - 1, E - 1, 3, False, True)
            rows_back(NC - 1)


_INS = ["x", "ctx_512", "L0_xattn_Wq", "L0_xattn_bq", "L0_xattn_Wk", "L0_xattn_bk", "L0_xattn_Wv", "L0_xattn_bv",
        "L0_xattn_Wo", "L0_xattn_bo", "L0_ffn_Wg", "L0_ffn_Wu", "L0_ffn_Wd"]


def kernel(**inputs):
    import numpy as np
    import concourse.bacc as bacc
    from concourse.bass_utils import run_bass_kernel_spmd

    nc = bacc.Bacc("TRN2", target_bir_lowering=False, num_devices=1)
    arrays, args = {}, []
    for name in _INS:
        a = np.ascontiguousarray(inputs[name])
        arrays[f"in_{name}"] = a
        args.append(nc.dram_tensor(f"in_{name}", a.shape, mybir.dt.from_np(a.dtype), kind="ExternalInput").ap())
    out = nc.dram_tensor("out_rows", inputs["x"].shape, F32, kind="ExternalOutput").ap()
    build(nc, *args, out)
    r = run_bass_kernel_spmd(nc, [arrays], core_ids=[0])
    return r.results[0]["out_rows"]
```

```python
from contextlib import ExitStack

import concourse.bass as bass
from concourse import mybir
from concourse.alu_op_type import AluOpType as ALU

F32 = mybir.dt.float32
BF16 = mybir.dt.bfloat16
F16 = mybir.dt.float16
I32 = mybir.dt.int32
F32R = mybir.dt.float32r
ACT = mybir.ActivationFunctionType
AX = mybir.AxisListType

P = 128
EPS = 1e-5
X_SCALE = 256.0
W_TOP = 2.0 ** 13


def build(nc, x, ctx_in, Wq, bq, Wk, bk, Wv, bv, Wo, bo, Wg, Wu, Wd, out):
    B, LQ, D = x.shape
    _, LK, DC = ctx_in.shape
    E, _, F = Wg.shape
    H = 16
    DH = D // H
    SCALE = float(DH) ** -0.5
    T = LQ // P
    NT = B * T
    R = 4
    J = H // R
    PAIRS = H // 2
    VC = 2 * DH + 2
    CB = 512 // LQ
    NC = B // CB
    CH = CB * LQ
    FT = F // P
    WE = FT * P
    KT_TILES = B * LK // P
    assert D == P and 2 * LK == P and FT == 4 and CH == 512 and NT == 16

    with ExitStack() as es:
        def sb(name, shape, dt=F32):
            return es.enter_context(nc.sbuf_tensor(name, shape, dt))

        def sem(name):
            return es.enter_context(nc.semaphore(name))

        x_sb = sb("x_sb", [P, NT, D])
        ctx_sb = sb("ctx_sb", [P, KT_TILES, DC])
        wq_sb = sb("wq_sb", [P, D])
        wk_sb = sb("wk_sb", [DC + 1, D])
        wv_sb = sb("wv_sb", [DC + 1, D])
        wo_sb = sb("wo_sb", [P, D])
        bq_sb = sb("bq_sb", [P, 1])
        bo_sb = sb("bo_sb", [P, D])
        w32 = sb("w32", [P, 3, E, WE])
        w16 = sb("w16", [P, 6, E, WE], F16)
        w_op = sb("w_op", [P, R, 3, 32])
        wk_op = sb("wk_op", [DC + 1, R, 3, 32])
        bq_op = sb("bq_op", [P, R])
        ident_op = sb("ident_op", [P, R, 3, 32])
        ident = sb("ident", [P, P])
        k_mask = sb("k_mask", [P, J])
        ones3 = sb("ones3", [3, P])
        half_c = sb("half_c", [P, 4])
        silu_c = sb("silu_c", [P, 4])
        bqs = sb("bqs", [P, 1])
        stats = sb("stats", [P, NT, 6])
        mv = sb("mv", [P, NT, 2])
        rstd = sb("rstd", [P, NT])
        vare = sb("vare", [P, NT])
        xn = sb("xn", [P, 8, D])
        xnT = [sb(f"xnT{i}", [P, CH]) for i in range(2)]
        xbo = x_sb
        x1 = x_sb
        xh = sb("xh", [P, NC, CH], F16)
        xl = sb("xl", [P, NC, CH], F16)
        ctxT = sb("ctxT", [DC + 1, B, 2, LK])
        q_hi = sb("q_hi", [P, B - CB, LQ], F32R)
        q_lo = sb("q_lo", [P, B - CB, LQ], F32R)
        q_all = w16[:, :, :, :].rearrange("p m e f -> p (m e f)").bitcast(F32R)[:, 0:R * (B - CB) * LQ].rearrange(
            "p (r b q) -> p r b q", r=R, b=B - CB)
        k_rows = sb("k_rows", [P, R, B, LK], F32R)
        v_res = sb("v_res", [P, B, PAIRS, DH])
        v_part = [sb(f"v_part{n}", [P, B, PAIRS, VC], BF16) for n in range(3)]
        q_op = sb("q_op", [P, 2, R, LQ], F32R)
        k_op = [sb(f"k_op{i}", [P, R, J * LK], F32R) for i in range(2)]
        nmax = [sb(f"nmax{i}", [P, 2, T, J]) for i in range(2)]
        nmax_parts = [sb(f"nmax_parts{i}", [P, 2, T, 32]) for i in range(2)]
        prob = [sb(f"prob{i}", [P, 4, LQ]) for i in range(2)]
        p_hi = [sb(f"p_hi{i}", [P, 4, LQ], F16) for i in range(2)]
        p_lo = [sb(f"p_lo{i}", [P, 4, LQ], F16) for i in range(2)]
        rsum = sb("rsum", [P, T, PAIRS, 2])
        o_sb = sb("o_sb", [P, T, H, DH])
        oT = sb("oT", [P, LQ])
        wmaxe = sb("wmaxe", [P, 3, E])
        wmax = sb("wmax", [P, 3])
        wmaxd = sb("wmaxd", [3, 4])
        wexp = sb("wexp", [P, 3])
        wscale = sb("wscale", [P, 3])
        fac = sb("fac", [P, 8])
        sg = [xnT[0][:, :], xnT[1][:, :]] + [sb(f"sg{i}", [P, CH])[:, :] for i in (2, 3)]
        h32 = [prob[i // 2][:, 2 * (i % 2):2 * (i % 2) + 2, :].rearrange("p r q -> p (r q)") for i in range(4)]
        hh = [p_hi[i // 2][:, 2 * (i % 2):2 * (i % 2) + 2, :].rearrange("p r q -> p (r q)") for i in range(4)]
        hl = [p_lo[i // 2][:, 2 * (i % 2):2 * (i % 2) + 2, :].rearrange("p r q -> p (r q)") for i in range(4)]
        yT = v_res[:, :, :, :].rearrange("p b r d -> p (b r d)")
        y_sb = [sb("y_sb", [P, CH])[:, :], xn[:, 4:8, :].rearrange("p t d -> p (t d)")]

        ps = es.enter_context(nc.psum_tensor("ps", [P, 8, 512], F32))
        s_table = sem("table_loaded")
        E_MID = E // 2
        ST_BANK, O_BANK = 4, 6
        XT_BANK = (6, 4, 6, 4)
        Q_BANK = (4, 5, 7, 6, 5, 7, 5)
        X2_BANK = (1, 5, 5, 5)
        U = 2 * B

        s_x = [sem(f"x_loaded{c}") for c in range(NC)]
        s_bo, s_rep = sem("bo_loaded"), sem("weight_columns_repeated")
        s_wsc = sem("weights_scaled")
        s_wme = sem("expert_weight_max")
        s_qall = [sem(f"query_rows_loaded{c}") for c in range(1, NC)]
        s_ctx, s_wq, s_small = sem("ctx_loaded"), sem("wq_loaded"), sem("small_loaded")
        s_w = [sem(f"ffn_weights_loaded{n}") for n in range(E // 2)]
        s_ident, s_cst, s_pset, s_vset, s_mask = (sem("identity_set"), sem("constants_set"), sem("operands_cleared"), sem("ones_set"),
                                                  sem("mask_set"))
        s_bq_ps, s_bqr, s_wv, s_wo = sem("bq_in_psum"), sem("bq_loaded"), sem("wv_loaded"), sem("wo_loaded")
        s_ctxT_ps, s_ctxT, s_kT_ps, s_v_ps = sem("ctxT_in_psum"), sem("ctxT_copied"), sem("kT_in_psum"), sem("v_in_psum")
        s_kh, s_kl = sem("k_hi_ready"), sem("k_lo_ready")
        s_v1, s_vr, s_v2, s_v3 = sem("v_part1"), sem("v_residue"), sem("v_part2"), sem("v_part3")
        s_bqs = sem("query_scaled")
        s_st, s_mv, s_ve, s_rstd, s_xn = sem("ln1_stats"), sem("ln1_mean_var"), sem("ln1_var_eps"), sem("ln1_rstd"), sem("ln1_rows")
        s_xnT_ps, s_xnT, s_xbo = sem("xnT_in_psum"), sem("xnT_copied"), sem("x_plus_bo")
        s_q_ps, s_qh, s_ql = sem("q_in_psum"), sem("q_hi_ready"), sem("q_lo_ready")
        s_qop = [[sem(f"q_operand_loaded{i}_{h}") for h in range(2)] for i in range(2)]
        s_kop = sem("k_operand_ready")
        s_s_ps, s_nm, s_nmh, s_nml = sem("scores_in_psum"), sem("max_ready"), sem("max_hi"), sem("max_parts")
        s_nmT_ps, s_nmT = sem("maxT_in_psum"), sem("maxT_copied")
        s_st_ps, s_p, s_ph, s_pl = sem("shifted_in_psum"), sem("prob_ready"), sem("prob_hi"), sem("prob_lo")
        s_o_ps, s_rs, s_o = sem("out_in_psum"), sem("sums_inverted"), sem("out_normed")
        s_oT_ps, s_oT, s_wo_ps, s_x1 = sem("oT_in_psum"), sem("oT_copied"), sem("wo_in_psum"), sem("x1_ready")
        s_wmax, s_wmT_ps, s_wm1, s_wd = sem("weight_max"), sem("weight_maxT_in_psum"), sem("weight_max_all"), sem("weight_max_diag")
        s_wb_ps, s_fac = sem("weight_max_in_psum"), sem("factors")
        s_wh, s_wl = sem("weights_hi"), sem("weights_lo")
        s_st2, s_mv2, s_ve2, s_rstd2, s_xn2 = sem("ln2_stats"), sem("ln2_mean_var"), sem("ln2_var_eps"), sem("ln2_rstd"), sem("ln2_rows")
        s_x2_ps, s_xh, s_xl = sem("x2T_in_psum"), sem("x2T_hi"), sem("x2T_lo")
        s_g, s_u, s_sg, s_h, s_hh, s_hl, s_d = (sem("gate_in_psum"), sem("up_in_psum"), sem("silu_ready"), sem("h_ready"),
                                                sem("h_hi"), sem("h_lo"), sem("down_added"))
        s_yT, s_y_ps, s_y, s_out = sem("yT_ready"), sem("y_in_psum"), sem("y_ready"), [sem(f"rows_stored{i}") for i in range(2)]

        x_view = x.rearrange("b (p t) d -> p b t d", t=T)
        out_view = out.rearrange("b (p t) d -> p b t d", t=T)
        x_by_b = x_sb[:, :, :].rearrange("p (b t) d -> p b t d", t=T)
        c_view = ctx_in.rearrange("(n m) k d -> (m k) n d", n=KT_TILES)
        w_view = [Wg.rearrange("e p f -> p e f"), Wu.rearrange("e p f -> p e f"),
                  Wd.rearrange("e (t p) d -> p e t d", p=P)]

        block = es.enter_context(nc.Block())

        @block.sync
        def _(sp):
            def rows(c):
                sp.dma_start(x_by_b[:, CB * c:CB * c + CB], x_view[:, CB * c:CB * c + CB]).then_inc(s_x[c], 16)

            def weights(e):
                for m in range(3):
                    dst = w32[:, m, e:e + 2, :]
                    if m == 2:
                        dst = dst.rearrange("p e (t d) -> p e t d", t=FT)
                    sp.dma_start(dst, w_view[m][:, e:e + 2]).then_inc(s_w[e // 2], 16)

            sp.dma_start(ctx_sb[:, :, :], c_view).then_inc(s_ctx, 16)
            rows(0)
            sp.dma_start(wk_sb[0:DC, :], Wk).then_inc(s_small, 16)
            sp.dma_start(wk_sb[DC:DC + 1, :], bk.rearrange("(a d) -> a d", a=1)).then_inc(s_small, 16)
            sp.dma_start(bq_sb[:, :], bq.rearrange("(d a) -> d a", a=1)).then_inc(s_bqr, 16)
            sp.dma_start(wq_sb[:, :], Wq).then_inc(s_wq, 16)
            rows(1)
            sp.dma_start(wv_sb[0:DC, :], Wv).then_inc(s_wv, 16)
            sp.dma_start(wv_sb[DC:DC + 1, :], bv.rearrange("(a d) -> a d", a=1)).then_inc(s_wv, 16)
            rows(2)
            rows(3)
            for e in range(0, E, 2):
                weights(e)
            sp.dma_start(bo_sb[:, :], bo.partition_broadcast(P)).then_inc(s_bo, 16)
            sp.dma_start(wo_sb[:, :], Wo).then_inc(s_wo, 16)

            def query_rows(c):
                sp.wait_ge(s_qh, R + c)
                sp.wait_ge(s_ql, R + c)
                for r in range(R):
                    rows, b0 = slice(32 * r, 32 * r + 32), CB * (c - 1)
                    for n, src in enumerate((q_hi, q_lo)):
                        sp.dma_start(q_all[32 * n:32 * n + 32, r, b0:b0 + CB, :].bitcast(F32),
                                     src[rows, b0:b0 + CB, :].bitcast(F32)).then_inc(s_qall[c - 1], 16)

            def query_operand(b, i, h):
                sp.wait_ge(s_st_ps, b * 2 + (h - 3))
                for to, rows in ((slice(0, 64), slice(0, 64)), (slice(64, 96), slice(0, 32))):
                    sp.dma_start(q_op[to, i, 2 * h:2 * h + 2, :].bitcast(F32),
                                 q_all[rows, 2 * h:2 * h + 2, bass.ds(b - CB, 1), :].rearrange("p r a q -> p r (a q)").bitcast(F32)
                                 ).then_inc(s_qop[i][h], 16)

            def chunk_operands(b):
                for i in range(2):
                    for h in range(2):
                        query_operand(b + i, i, h)

            query_rows(1)
            sp.wait_ge(s_qall[0], 16 * 2 * R)
            query_operand(2, 0, 0)
            query_operand(2, 0, 1)
            query_rows(2)
            query_operand(3, 1, 0)
            query_operand(3, 1, 1)
            query_rows(3)
            for c in range(2, NC):
                sp.wait_ge(s_qall[c - 1], 16 * 2 * R)
                chunk_operands(CB * c)
            for c in range(NC):
                sp.wait_ge(s_y, c + 1)
                sp.dma_start(out_view[:, CB * c:CB * c + CB],
                             y_sb[c % 2].rearrange("p (b t d) -> p b t d", b=CB, t=T)).then_inc(s_out[c % 2], 16)
            for i in range(2):
                sp.wait_ge(s_out[i], 16 * NC // 2)

        @block.gpsimd
        def _(pool):
            pool.memset(ident[:, :], 0.0).then_inc(s_cst, 1)
            pool.wait_ge(s_cst, 1)
            pool.affine_select(out=ident[:, :], in_=ident[:, :], compare_op=ALU.not_equal, fill=1.0, base=0,
                               pattern=[[-1, P]], channel_multiplier=1).then_inc(s_ident, 1)
            pool.memset(half_c[:, :], -0.5).then_inc(s_cst, 1)
            pool.memset(k_rows[:, :, :, :].bitcast(F32), 1.0).then_inc(s_pset, 1)
            for n in range(3):
                pool.memset(v_part[n][:, :, :, :].rearrange("p b r c -> p (b r c)").bitcast(F32), 0.0).then_inc(s_pset, 1)
            for i in range(2):
                pool.memset(nmax_parts[i][:, :, :, :], 0.0).then_inc(s_pset, 1)
            pool.wait_ge(s_cst, 2)
            def root(c):
                pool.wait_ge(s_ve, c + 1)
                pool.tensor_tensor(rstd[:, 4 * c:4 * c + 4], vare[:, 4 * c:4 * c + 4], half_c[:, :], ALU.pow).then_inc(s_rstd, 1)

            def add_bo(c):
                pool.wait_ge(s_xn, 4 * c + 4)
                pool.tensor_tensor(xbo[:, 4 * c:4 * c + 4, :], x_sb[:, 4 * c:4 * c + 4, :],
                                   bo_sb[:, :].unsqueeze(1).to_broadcast([P, 4, D]), ALU.add).then_inc(s_xbo, 1)

            def norm_rows(c):
                if c >= 2:
                    pool.wait_ge(s_xnT_ps, c - 1)
                pool.wait_ge(s_rstd, c + 1)
                for t in range(4 * c, 4 * c + 4):
                    pool.tensor_scalar(xn[:, t % 8, :], x_sb[:, t, :], mv[:, t, 0:1], rstd[:, t:t + 1], ALU.subtract, ALU.mult).then_inc(s_xn, 1)

            def key_operand(u, b, i, h, reuse):
                if reuse:
                    pool.wait_ge(s_st_ps, u - 3)
                pool.tensor_tensor(k_op[i][:, 2 * h:2 * h + 2, :].rearrange("p r (j k) -> p r j k", j=J),
                                   k_rows[:, 2 * h:2 * h + 2, bass.ds(b, 1), :].bitcast(F32).to_broadcast([P, 2, J, LK]),
                                   k_mask[:, :].unsqueeze(1).unsqueeze(3).to_broadcast([P, 2, J, LK]), ALU.mult).then_inc(s_kop, 1)

            for c in range(NC):
                root(c)
            pool.wait_ge(s_xn, 12)
            norm_rows(3)
            pool.wait_ge(s_kop, 2)
            for u in range(2, 4):
                key_operand(u, 1, 1, u % 2, False)
            pool.wait_ge(s_bo, 16)
            for c in range(NC):
                add_bo(c)

            def prob_low(u, h, reuse):
                pool.wait_ge(s_ph, u + 1)
                if reuse:
                    pool.wait_ge(s_o_ps, u - 1)
                pool.tensor_tensor(p_lo[h][:, :, :], prob[h][:, :, :], p_hi[h][:, :, :], ALU.subtract).then_inc(s_pl, 1)

            for u in range(4):
                prob_low(u, u % 2, u >= 2)
            pool.wait_ge(s_kop, 8)
            with pool.Fori(1, U // 4 - 1) as n:
                for v in range(4):
                    key_operand(n * 4 + (v + 4), n * 2 + (v // 2 + 2), v // 2, v % 2, True)
                    prob_low(n * 4 + v, v % 2, True)

            def root2(c):
                pool.wait_ge(s_ve2, c + 1)
                pool.tensor_tensor(rstd[:, 4 * c:4 * c + 4], vare[:, 4 * c:4 * c + 4], half_c[:, :], ALU.pow).then_inc(s_rstd2, 1)

            def weights_low(e):
                for m in range(3):
                    pool.wait_ge(s_wh, e * 3 + (m + 1))
                    pool.tensor_tensor(w16[:, 3 + m, bass.ds(e, 1), :], w32[:, m, bass.ds(e, 1), :], w16[:, m, bass.ds(e, 1), :],
                                       ALU.subtract).then_inc(s_wl, 1)

            root2(0)
            for u in range(U - 4, U):
                prob_low(u, u % 2, True)

            def rows2(c):
                pool.wait_ge(s_rstd2, c + 1)
                pool.wait_ge(s_x2_ps, c)
                for t in range(4):
                    pool.tensor_scalar(xn[:, t, :], x1[:, c * 4 + t, :], mv[:, t, 0:1], rstd[:, c * 4 + t:c * 4 + t + 1],
                                       ALU.subtract, ALU.mult).then_inc(s_xn2, 1)

            with pool.Fori(1, E_MID + 2) as e:
                weights_low(e)
            root2(1)
            rows2(1)
            with pool.Fori(E_MID + 2, E) as e:
                weights_low(e)
            for c in range(2, NC):
                root2(c)
                rows2(c)

        @block.scalar
        def _(act):
            act.wait_ge(s_cst, 2)
            nc.scalar.activation(silu_c[:, :], half_c[:, :], ACT.Exp).then_inc(s_table, 1)
            act.wait_ge(s_ctxT_ps, 1)
            for m in range(2):
                nc.scalar.copy(ctxT[0:DC, :, m, :], ps[0:DC, 7, :].rearrange("p (b k) -> p b k", k=LK)).then_inc(s_ctxT, 1)
            act.wait_ge(s_wq, 16)
            nc.scalar.mul(w_op[:, :, :, :], wq_sb[:, :].rearrange("p (r a d) -> p r a d", r=R, a=1).to_broadcast([P, R, 3, 32]), SCALE).then_inc(s_bqs, 1)

            def key_high(r):
                act.wait_ge(s_kT_ps, r + 1)
                if r == 0:
                    act.wait_ge(s_pset, 1)
                nc.scalar.copy(k_rows[0:3 * 32, r, :, :], ps[0:3 * 32, r, :].rearrange("p (b k) -> p b k", k=LK)).then_inc(s_kh, 1)

            def rows_T(c):
                act.wait_ge(s_xnT_ps, c + 1)
                nc.scalar.copy(xnT[c % 2][:, :], ps[:, XT_BANK[c], :]).then_inc(s_xnT, 1)

            def query_high(c):
                act.wait_ge(s_q_ps, R + c)
                nc.scalar.activation(q_hi[:, CB * (c - 1):CB * c, :], ps[:, Q_BANK[R + c - 1], :].rearrange("p (b q) -> p b q", q=LQ),
                                     ACT.Identity, bias=bqs[:, 0:1]).then_inc(s_qh, 1)

            def first_query_high(r):
                act.wait_ge(s_q_ps, r + 1)
                nc.scalar.activation(q_op[0:3 * 32, :, r, :], ps[0:3 * 32, Q_BANK[r], :].rearrange("p (b q) -> p b q", q=LQ),
                                     ACT.Identity, bias=bq_op[0:3 * 32, r:r + 1]).then_inc(s_qh, 1)

            key_high(0)
            act.wait_ge(s_bq_ps, 1)
            nc.scalar.mul(bq_op[0:3 * 32, :], ps[0:3 * 32, 4, 0:R], SCALE).then_inc(s_bqs, 1)
            key_high(1)
            rows_T(0)
            nc.scalar.mul(bqs[:, :], bq_sb[:, :], SCALE).then_inc(s_bqs, 1)
            act.wait_ge(s_bqs, 2)
            nc.scalar.mul(wq_sb[:, :], wq_sb[:, :], SCALE).then_inc(s_bqs, 1)
            key_high(2)
            key_high(3)
            act.wait_ge(s_bqs, 4)
            for r in range(R):
                first_query_high(r)
            rows_T(1)
            act.wait_ge(s_v_ps, 1)
            act.wait_ge(s_pset, 4)
            for n in range(2):
                for j in range(2):
                    half = slice(LK * j, LK * j + LK)
                    nc.scalar.copy(v_part[0][half, 4 * n:4 * n + 4, :, DH * j:DH * j + DH].rearrange("p b r d -> p (b r) d"),
                                   ps[half, 2 + n, :].rearrange("p (r j d) -> p r j d", j=2, d=DH)[:, :, j, :]).then_inc(s_v1, 1)
            query_high(1)
            rows_T(2)
            query_high(2)

            def shift_rows(u, i, h):
                act.wait_ge(s_nmT_ps, u + 1)
                nc.scalar.copy(q_op[3 * 32:P, i, 2 * h:2 * h + 2, :],
                               ps[0:32, 2 * h, :].rearrange("p (r q) -> p r q", r=2)).then_inc(s_nmT, 1)

            shift_rows(0, 0, 0)
            rows_T(3)
            query_high(3)
            act.wait_ge(s_vr, 4)
            for j in range(2):
                half = slice(LK * j, LK * j + LK)
                nc.scalar.copy(v_part[1][half, :, :, DH * j:DH * j + DH].rearrange("p b r d -> p (b r) d"),
                               v_res[half, :, :, :].rearrange("p b r d -> p (b r) d")).then_inc(s_v2, 1)

            def exps(u, h, reuse):
                act.wait_ge(s_st_ps, u + 1)
                if reuse:
                    act.wait_ge(s_pl, u - 1)
                nc.scalar.activation(prob[h][:, :, :], ps[:, ST_BANK:ST_BANK + 2, :].rearrange("p r (t q) -> p (r t) q", t=2),
                                     ACT.Exp).then_inc(s_p, 1)

            def high_part(u, h, reuse):
                act.wait_ge(s_p, u + 1)
                if reuse:
                    act.wait_ge(s_o_ps, u - 1)
                nc.scalar.copy(p_hi[h][:, :, :], prob[h][:, :, :]).then_inc(s_ph, 1)

            def out_T(b, i):
                act.wait_ge(s_oT_ps, b + 1)
                nc.scalar.copy(oT[:, :], ps[:, O_BANK + i, 0:LQ]).then_inc(s_oT, 1)

            def slot(u, b, v, at):
                exps(u, v % 2, at >= 2)
                if at + 1 < U:
                    shift_rows(u + 1, (v + 1) // 2 % 2, (v + 1) % 2)
                if v % 2 == 0 and at >= 4:
                    out_T(b - 2, v // 2)
                high_part(u, v % 2, at >= 2)

            def rows_high(c):
                act.wait_ge(s_x2_ps, c + 1)
                nc.scalar.activation(xh[:, c, :], ps[:, X2_BANK[c], :], ACT.Copy, scale=X_SCALE).then_inc(s_xh, 1)

            for u in range(4):
                slot(u, u // 2, u, u)
            with act.Fori(1, U // 4 - 1) as n:
                for v in range(4):
                    slot(n * 4 + v, n * 2 + v // 2, v, 4 + v)
            def weights(e):
                for m in range(3):
                    weight_high(m, e)

            def weight_high(m, e):
                act.wait_ge(s_wsc, e * 3 + (m + 1))
                nc.scalar.copy(w16[:, m, bass.ds(e, 1), :], w32[:, m, bass.ds(e, 1), :]).then_inc(s_wh, 1)

            slot(U - 4, B - 2, 0, U - 4)
            slot(U - 3, B - 2, 1, U - 3)
            slot(U - 2, B - 1, 2, U - 2)
            exps(U - 1, 1, True)
            weights(0)
            rows_high(0)
            high_part(U - 1, 1, True)
            act.wait_ge(s_table, 1)
            nc.scalar.activation(silu_c[:, :], half_c[:, :], ACT.Silu).then_inc(s_table, 1)

            def silu(i, u):
                act.wait_ge(s_g, i + 1)
                nc.scalar.activation(sg[u], ps[:, u % 2, :], ACT.Silu, scale=fac[:, 0:1]).then_inc(s_sg, 1)

            def high(i, u):
                act.wait_ge(s_h, i + 1)
                nc.scalar.copy(hh[u], h32[u]).then_inc(s_hh, 1)

            def y_out(c):
                act.wait_ge(s_d, (c + 1) * (E * FT))
                if c > 0:
                    act.wait_ge(s_y_ps, c)
                nc.scalar.activation(yT, ps[:, 4, :], ACT.Copy, scale=fac[:, 2:3]).then_inc(s_yT, 1)

            def body(e, fresh, split=False, after=None):
                for u in range(FT):
                    i = e * FT + u
                    if not fresh:
                        act.wait_ge(s_h, i - 3)
                    silu(i, u)
                    if fresh and u == 0:
                        out_T(B - 2, 0)
                    if fresh and u == 3:
                        act.wait_ge(s_o_ps, U)
                    if not (fresh and u == 0):
                        if not fresh:
                            act.wait_ge(s_d, i - 4)
                        high(i - 1, (u - 1) % 4)
                    if split and u < 3:
                        weight_high(u, e + 1)
                    if after is not None and u == 1:
                        y_out(after)

            body(0, True, True)
            out_T(B - 1, 1)
            with act.Fori(1, E_MID + 2) as e:
                body(e, False, True)
            rows_high(1)
            with act.Fori(E_MID + 2, E - 1) as e:
                body(e, False, True)
            body(E - 1, False)
            for c in range(1, NC):
                body(E * c, False, after=c - 1)
                with act.Fori(E * c + 1, E * c + E_MID + 2) as e:
                    body(e, False)
                if c + 1 < NC:
                    rows_high(c + 1)
                with act.Fori(E * c + E_MID + 2, E * c + E) as e:
                    body(e, False)
            act.wait_ge(s_d, NC * E * FT - 4)
            high(NC * E * FT - 1, 3)
            y_out(NC - 1)

        @block.vector
        def _(dve):
            nc.vector.memset(ctxT[DC:DC + 1, :, :, :], 1.0).then_inc(s_vset, 1)
            nc.vector.memset(ones3[:, :], 1.0).then_inc(s_vset, 1)
            dve.wait_ge(s_ident, 1)
            nc.vector.tensor_copy(ident_op[:, :, :, :], ident[:, :].rearrange("p (r a d) -> p r a d", r=R, a=1).to_broadcast([P, R, 3, 32])).then_inc(s_rep, 1)
            nc.vector.tensor_reduce(k_mask[0:3 * 32, :], ident[0:3 * 32, :].rearrange("p (a j d) -> p j a d", j=J, d=DH), AX.XY, ALU.add).then_inc(s_mask, 1)
            nc.vector.tensor_reduce(k_mask[3 * 32:P, :], ident[3 * 32:P, :].rearrange("p (n c) -> p c n", c=J), AX.X, ALU.add).then_inc(s_mask, 1)
            def norm_stats(c):
                dve.wait_ge(s_x[c], 16)
                for t in range(4 * c, 4 * c + 4):
                    nc.vector.bn_stats(stats[:, t, :], x_sb[:, t, :]).then_inc(s_st, 1)
                for t in range(4 * c, 4 * c + 4):
                    dve.wait_ge(s_st, t + 1)
                    nc.vector.bn_aggr(mv[:, t, :], stats[:, t, :]).then_inc(s_mv, 1)
                dve.wait_ge(s_mv, 4 * c + 4)
                nc.vector.tensor_scalar(vare[:, 4 * c:4 * c + 4], mv[:, 4 * c:4 * c + 4, 1], EPS, None, ALU.add).then_inc(s_ve, 1)

            def norm_rows(c):
                dve.wait_ge(s_rstd, c + 1)
                if c >= 2:
                    dve.wait_ge(s_xnT_ps, c - 1)
                for t in range(4 * c, 4 * c + 4):
                    nc.vector.tensor_scalar(xn[:, t % 8, :], x_sb[:, t, :], mv[:, t, 0:1], rstd[:, t:t + 1], ALU.subtract, ALU.mult).then_inc(s_xn, 1)

            def key_low(r):
                dve.wait_ge(s_kh, r + 1)
                nc.vector.tensor_tensor(k_rows[64:96, r, :, :], ps[64:96, r, :].rearrange("p (b k) -> p b k", k=LK),
                                        k_rows[64:96, r, :, :].bitcast(F32), ALU.subtract).then_inc(s_kl, 1)

            def first_query_low(r):
                dve.wait_ge(s_qh, r + 1)
                nc.vector.scalar_tensor_tensor(out=q_op[32:64, :, r, :], in0=ps[32:64, Q_BANK[r], :].rearrange("p (b q) -> p b q", q=LQ),
                                               scalar=bq_op[32:64, r:r + 1], in1=q_op[32:64, :, r, :].bitcast(F32),
                                               op0=ALU.add, op1=ALU.subtract).then_inc(s_ql, 1)

            def query_low(c):
                dve.wait_ge(s_qh, R + c)
                nc.vector.scalar_tensor_tensor(out=q_lo[:, CB * (c - 1):CB * c, :], in0=ps[:, Q_BANK[R + c - 1], :].rearrange("p (b q) -> p b q", q=LQ),
                                               scalar=bqs[:, 0:1], in1=q_hi[:, CB * (c - 1):CB * c, :].bitcast(F32),
                                               op0=ALU.add, op1=ALU.subtract).then_inc(s_ql, 1)

            def key_operand(u, b, i, h, reuse):
                if reuse:
                    dve.wait_ge(s_st_ps, u - 3)
                nc.vector.tensor_tensor(k_op[i][:, 2 * h:2 * h + 2, :].rearrange("p r (j k) -> p r j k", j=J),
                                        k_rows[:, 2 * h:2 * h + 2, bass.ds(b, 1), :].bitcast(F32).to_broadcast([P, 2, J, LK]),
                                        k_mask[:, :].unsqueeze(1).unsqueeze(3).to_broadcast([P, 2, J, LK]), ALU.mult).then_inc(s_kop, 1)

            def value_residue():
                dve.wait_ge(s_v1, 4)
                for n in range(2):
                    for j in range(2):
                        half = slice(LK * j, LK * j + LK)
                        nc.vector.tensor_tensor(v_res[half, 4 * n:4 * n + 4, :, :].rearrange("p b r d -> p (b r) d"),
                                                ps[half, 2 + n, :].rearrange("p (r j d) -> p r j d", j=2, d=DH)[:, :, j, :],
                                                v_part[0][half, 4 * n:4 * n + 4, :, DH * j:DH * j + DH].rearrange("p b r d -> p (b r) d"),
                                                ALU.subtract).then_inc(s_vr, 1)

            def value_last():
                dve.wait_ge(s_v2, 2)
                for j in range(2):
                    half = slice(LK * j, LK * j + LK)
                    nc.vector.tensor_tensor(v_part[2][half, :, :, DH * j:DH * j + DH].rearrange("p b r d -> p (b r) d"),
                                            v_res[half, :, :, :].rearrange("p b r d -> p (b r) d"),
                                            v_part[1][half, :, :, DH * j:DH * j + DH].rearrange("p b r d -> p (b r) d"),
                                            ALU.subtract).then_inc(s_v3, 1)

            def row_max(u, h):
                dve.wait_ge(s_s_ps, u + 1)
                nc.vector.tensor_reduce(nmax[h][:, :, :, :], ps[:, 2 * h:2 * h + 2, :].rearrange("p r (t j k) -> p (r t j) k", t=T, j=J),
                                        AX.X, ALU.max, negate=True).then_inc(s_nm, 1)
                dve.wait_ge(s_nm, u + 1)
                hi, lo = nmax_parts[h][:, :, :, 0:J], nmax_parts[h][:, :, :, J:2 * J]
                nc.vector.tensor_copy(hi.bitcast(F32R), nmax[h][:, :, :, :]).then_inc(s_nmh, 1)
                dve.wait_ge(s_nmh, u + 1)
                nc.vector.tensor_tensor(lo, nmax[h][:, :, :, :], hi, ALU.subtract).then_inc(s_nml, 1)

            def norm_out(b, i):
                dve.wait_ge(s_o_ps, b * 2 + 2)
                o_ps = ps[:, O_BANK + i, 0:T * PAIRS * VC].rearrange("p (t r c) -> p t r c", t=T, c=VC)
                nc.vector.reciprocal(rsum[:, :, :, :], o_ps[:, :, :, 2 * DH:VC]).then_inc(s_rs, 1)
                dve.wait_ge(s_rs, b + 1)
                for t in range(T):
                    nc.vector.tensor_tensor(o_sb[:, t, :, :].rearrange("p (r j) d -> p r j d", j=2),
                                            o_ps[:, t, :, 0:2 * DH].rearrange("p r (j d) -> p r j d", j=2),
                                            rsum[:, t, :, :].unsqueeze(3).to_broadcast([P, PAIRS, 2, DH]), ALU.mult).then_inc(s_o, 1)

            def residual(b, i):
                dve.wait_ge(s_wo_ps, b + 1)
                nc.vector.tensor_tensor(x1[:, bass.ds(b * T, T), :], ps[:, O_BANK + i, LQ:2 * LQ].rearrange("p (t d) -> p t d", t=T),
                                        xbo[:, bass.ds(b * T, T), :], ALU.add).then_inc(s_x1, 1)

            def weight_scale(m, e):
                nc.vector.tensor_scalar(w32[:, m, bass.ds(e, 1), :], w32[:, m, bass.ds(e, 1), :], wscale[:, m:m + 1], None, ALU.mult).then_inc(s_wsc, 1)

            def weight_low(m):
                dve.wait_ge(s_wh, m + 1)
                nc.vector.tensor_tensor(w16[:, 3 + m, 0, :], w32[:, m, 0, :], w16[:, m, 0, :], ALU.subtract).then_inc(s_wl, 1)

            def norm2(c):
                dve.wait_ge(s_x1, CB * (c + 1))
                for t in range(4):
                    nc.vector.bn_stats(stats[:, t, :], x1[:, c * 4 + t, :]).then_inc(s_st2, 1)
                dve.wait_ge(s_st2, c * 4 + 4)
                for t in range(4):
                    nc.vector.bn_aggr(mv[:, t, :], stats[:, t, :]).then_inc(s_mv2, 1)
                dve.wait_ge(s_mv2, c * 4 + 4)
                nc.vector.tensor_scalar(vare[:, 4 * c:4 * c + 4], mv[:, 0:4, 1], EPS, None, ALU.add).then_inc(s_ve2, 1)

            def norm2_rows(c):
                dve.wait_ge(s_rstd2, c + 1)
                for t in range(4):
                    nc.vector.tensor_scalar(xn[:, t, :], x1[:, c * 4 + t, :], mv[:, t, 0:1], rstd[:, c * 4 + t:c * 4 + t + 1],
                                            ALU.subtract, ALU.mult).then_inc(s_xn2, 1)

            def rows_low(c):
                dve.wait_ge(s_xh, c + 1)
                nc.vector.scalar_tensor_tensor(out=xl[:, c, :], in0=ps[:, X2_BANK[c], :], scalar=X_SCALE,
                                               in1=xh[:, c, :], op0=ALU.mult, op1=ALU.subtract).then_inc(s_xl, 1)

            def weights_max(e):
                nc.vector.tensor_reduce(wmaxe[:, :, bass.ds(e, 1)], w32[:, :, bass.ds(e, 1), :], AX.X, ALU.max,
                                        apply_absolute_value=True).then_inc(s_wme, 1)

            def slot(u, b, v, at):
                if v % 2 == 1 and at >= 3:
                    norm_out(b - 1, 1 - v // 2)
                if at < 4:
                    key_operand(u + 4, b + 2, v // 2, v % 2, True)
                if at + 3 < U:
                    row_max(u + 3, 1 - v % 2)
                if v % 2 == 0 and at >= 4:
                    residual(b - 2, v // 2)

            norm_stats(0)
            dve.wait_ge(s_small, 32)
            nc.vector.tensor_copy(wk_op[:, :, :, :], wk_sb[:, :].rearrange("p (r a d) -> p r a d", r=R, a=1).to_broadcast([DC + 1, R, 3, 32])).then_inc(s_rep, 1)
            dve.wait_ge(s_pset, 4)
            for j in range(2):
                nc.vector.memset(v_part[0][LK * j:LK * j + LK, :, :, 2 * DH + j], 1.0).then_inc(s_vset, 1)
            norm_rows(0)
            key_low(0)
            norm_stats(1)
            key_low(1)
            norm_stats(2)
            key_low(2)
            norm_rows(1)
            key_low(3)
            dve.wait_ge(s_mask, 2)
            dve.wait_ge(s_kl, R)
            key_operand(0, 0, 0, 0, False)
            norm_stats(3)
            first_query_low(0)
            first_query_low(1)
            first_query_low(2)
            first_query_low(3)
            norm_rows(2)
            dve.wait_ge(s_pset, 6)
            row_max(0, 0)
            key_operand(1, 0, 0, 1, False)
            query_low(1)
            value_residue()
            query_low(2)
            query_low(3)
            row_max(1, 1)
            value_last()
            dve.wait_ge(s_kop, 4)
            row_max(2, 0)
            for n in range(E // 2):
                dve.wait_ge(s_w[n], 48)
            for u in range(4):
                slot(u, u // 2, u, u)
                if u > 0:
                    weights_max(u - 1)
            dve.wait_ge(s_xbo, NC)
            with dve.Fori(1, U // 4 - 1) as n:
                for v in range(4):
                    slot(n * 4 + v, n * 2 + v // 2, v, 4 + v)
                    if v % 2 == 0:
                        weights_max(n * 2 + (v // 2 + 1))
            norm2(0)
            slot(U - 4, B - 2, 0, U - 4)
            weights_max(E - 1)
            slot(U - 3, B - 2, 1, U - 3)
            dve.wait_ge(s_wme, E)
            nc.vector.tensor_reduce(wmax[:, :], wmaxe[:, :, :], AX.X, ALU.max).then_inc(s_wmax, 1)
            dve.wait_ge(s_wmT_ps, 1)
            nc.vector.tensor_reduce(wmaxd[:, 3:4], ps[0:3, 0, 0:P], AX.X, ALU.max).then_inc(s_wm1, 1)
            dve.wait_ge(s_wm1, 1)
            nc.vector.tensor_scalar(wmaxd[:, 0:3], ident[0:3, 0:3], wmaxd[:, 3:4], None, ALU.mult).then_inc(s_wd, 1)
            norm2_rows(0)
            dve.wait_ge(s_wb_ps, 1)
            nc.vector.tensor_scalar(wmax[:, :], ps[:, 0, LQ:LQ + 3], 1e-30, 1e30, ALU.max, ALU.min).then_inc(s_wm1, 1)
            dve.wait_ge(s_wm1, 2)
            nc.vector.tensor_scalar(wexp[:, :].bitcast(I32), wmax[:, :].bitcast(I32), 0x7F800000, None, ALU.bitwise_and).then_inc(s_wm1, 1)
            dve.wait_ge(s_wm1, 3)
            nc.vector.reciprocal(fac[:, 4:7], wexp[:, :]).then_inc(s_wm1, 1)
            dve.wait_ge(s_wm1, 4)
            nc.vector.tensor_scalar(wscale[:, :], fac[:, 4:7], W_TOP, None, ALU.mult).then_inc(s_wm1, 1)
            nc.vector.tensor_scalar(fac[:, 0:1], wexp[:, 0:1], 1.0 / (W_TOP * X_SCALE), None, ALU.mult).then_inc(s_wm1, 1)
            nc.vector.tensor_scalar(fac[:, 1:2], fac[:, 4:5], 0.5 / (W_TOP * X_SCALE), None, ALU.mult).then_inc(s_wm1, 1)
            nc.vector.tensor_scalar(fac[:, 3:4], wexp[:, 0:1], wexp[:, 1:2], 2.0 / W_TOP, ALU.mult, ALU.mult).then_inc(s_wm1, 1)
            dve.wait_ge(s_wm1, 8)
            nc.vector.tensor_scalar(fac[:, 2:3], fac[:, 3:4], wexp[:, 2:3], None, ALU.mult).then_inc(s_fac, 1)

            dve.wait_ge(s_fac, 1)
            weight_scale(0, 0)
            weight_scale(1, 0)
            weight_scale(2, 0)
            slot(U - 2, B - 1, 2, U - 2)
            weight_low(0)
            weight_low(1)
            rows_low(0)
            weight_low(2)
            slot(U - 1, B - 1, 3, U - 1)

            def hidden(i, u):
                dve.wait_ge(s_u, i + 1)
                dve.wait_ge(s_sg, i + 1)
                nc.vector.scalar_tensor_tensor(out=h32[u], in0=ps[:, 2 + u % 2, :], scalar=fac[:, 1:2],
                                               in1=sg[u], op0=ALU.mult, op1=ALU.mult).then_inc(s_h, 1)

            def low(i, u):
                dve.wait_ge(s_hh, i + 1)
                nc.vector.tensor_tensor(hl[u], h32[u], hh[u], ALU.subtract).then_inc(s_hl, 1)

            def y_add(c):
                dve.wait_ge(s_y_ps, c + 1)
                if c >= 2:
                    dve.wait_ge(s_out[c % 2], 16 * (c // 2))
                nc.vector.tensor_tensor(y_sb[c % 2].rearrange("p (t d) -> p t d", d=D), ps[:, 6, :].rearrange("p (t d) -> p t d", d=D),
                                        x1[:, 4 * c:4 * c + 4, :], ALU.add).then_inc(s_y, 1)

            def body(e, fresh=False, c=None, split=False):
                for u in range(FT):
                    i = e * FT + u
                    if split and u < 3:
                        weight_scale(u, e + 1)
                    if fresh and u == 2:
                        dve.wait_ge(s_pl, U)
                    hidden(i, u)
                    if not (fresh and u == 0):
                        if fresh and u == 3:
                            dve.wait_ge(s_o_ps, U)
                        low(i - 1, (u - 1) % 4)
                    if c is not None:
                        if fresh and u == 2:
                            residual(B - 2, 0)
                            norm_out(B - 1, 1)
                if c is not None:
                    if c > 0:
                        y_add(c - 1)

            body(0, True, 0, True)
            residual(B - 1, 1)
            with dve.Fori(1, E_MID) as e:
                body(e, split=True)
            norm2(1)
            with dve.Fori(E_MID, E_MID + 2) as e:
                body(e, split=True)
            rows_low(1)
            with dve.Fori(E_MID + 2, E - 1) as e:
                body(e, split=True)
            body(E - 1)
            for c in range(1, NC):
                body(E * c, False, c)
                with dve.Fori(E * c + 1, E * c + E_MID) as e:
                    body(e)
                if c + 1 < NC:
                    norm2(c + 1)
                with dve.Fori(E * c + E_MID, E * c + E_MID + 2) as e:
                    body(e)
                if c + 1 < NC:
                    rows_low(c + 1)
                with dve.Fori(E * c + E_MID + 2, E * c + E) as e:
                    body(e)
            low(NC * E * FT - 1, 3)
            y_add(NC - 1)

        @block.tensor
        def _(pe):
            pe.wait_ge(s_ident, 1)
            def warm(count):
                for _ in range(count):
                    nc.tensor.transpose(ps[:, 5, 0:P], ident[:, :], ident[:, :])

            warm(12)
            pe.wait_ge(s_ctx, 16)
            for n in range(KT_TILES):
                mm = nc.tensor.transpose(ps[0:DC, 7, P * n:P * n + P], ctx_sb[:, n, :], ident[:, :])
            mm.then_inc(s_ctxT_ps, 1)

            warm(7)

            def bias_rows():
                pe.wait_ge(s_bqr, 16)
                for r in range(R):
                    mm = nc.tensor.matmul(ps[0:3 * 32, 4, r:r + 1], ident_op[:, r, :, :].rearrange("p a d -> p (a d)"), bq_sb[:, :], start=True, stop=True)
                mm.then_inc(s_bq_ps, 1)

            def keys(r):
                nc.tensor.matmul(ps[0:3 * 32, r, :], wk_op[:, r, :, :].rearrange("p a d -> p (a d)"), ctxT[:, :, 0, :], start=True, stop=True).then_inc(s_kT_ps, 1)

            def rows_T(c):
                pe.wait_ge(s_xn, 4 * c + 4)
                for t in range(4):
                    mm = nc.tensor.transpose(ps[:, XT_BANK[c], P * t:P * t + P], xn[:, (4 * c + t) % 8, :], ident[:, :])
                mm.then_inc(s_xnT_ps, 1)

            def first_queries(r):
                nc.tensor.matmul(ps[0:3 * 32, Q_BANK[r], :], w_op[:, r, :, :].rearrange("p a d -> p (a d)"), xnT[0][:, :], start=True, stop=True).then_inc(s_q_ps, 1)

            def queries(c):
                pe.wait_ge(s_xnT, c + 1)
                nc.tensor.matmul(ps[:, Q_BANK[R + c - 1], :], wq_sb[:, :], xnT[c % 2][:, :], start=True, stop=True).then_inc(s_q_ps, 1)

            def scores(u, i, h, reuse):
                pe.wait_ge(s_kop, u + 1)
                if reuse:
                    pe.wait_ge(s_nmT, u - 1)
                for t in range(T):
                    for r in range(2):
                        mm = nc.tensor.matmul(ps[:, 2 * h + r, J * LK * t:J * LK * (t + 1)], q_op[0:3 * 32, i, 2 * h + r, P * t:P * t + P],
                                              k_op[i][0:3 * 32, 2 * h + r, :], start=True, stop=True)
                mm.then_inc(s_s_ps, 1)

            def maxima_T(u, h):
                pe.wait_ge(s_nml, u + 1)
                for r in range(2):
                    for t in range(T):
                        mm = nc.tensor.transpose(ps[0:32, 2 * h, LQ * r + P * t:LQ * r + P * t + P], nmax_parts[h][:, r, t, :], ident[:, :])
                mm.then_inc(s_nmT_ps, 1)

            def shifted(u, i, h, reuse):
                pe.wait_ge(s_nmT, u + 1)
                if reuse:
                    pe.wait_ge(s_p, u)
                for r in range(2):
                    for t in range(2):
                        mm = nc.tensor.matmul(ps[:, ST_BANK + r, LQ * t:LQ * t + LQ], k_op[i][:, 2 * h + r, P * t:P * t + P],
                                              q_op[:, i, 2 * h + r, :], start=True, stop=True)
                mm.then_inc(s_st_ps, 1)

            def values(u, b, i, h, reuse):
                pe.wait_ge(s_ph, u + 1)
                pe.wait_ge(s_pl, u + 1)
                if reuse and h == 0:
                    pe.wait_ge(s_x1, b - 1)
                for t in range(T):
                    for r in range(4):
                        c0 = (t * PAIRS + 4 * h + r) * VC
                        terms = [(p_hi, 0), (p_hi, 1), (p_hi, 2), (p_lo, 0), (p_lo, 1), (p_lo, 2)]
                        for k, (part, n) in enumerate(terms):
                            mm = nc.tensor.matmul(ps[:, O_BANK + i, c0:c0 + VC], part[h][:, r, P * t:P * t + P],
                                                  v_part[n][:, bass.ds(b, 1), 4 * h + r, :].rearrange("p a c -> p (a c)"),
                                                  start=(k == 0), stop=(k == len(terms) - 1))
                mm.then_inc(s_o_ps, 1)

            def out_T(b, i):
                pe.wait_ge(s_o, b * T + T)
                for t in range(T):
                    mm = nc.tensor.transpose(ps[:, O_BANK + i, P * t:P * t + P], o_sb[:, t, :, :].rearrange("p h d -> p (h d)"), ident[:, :])
                mm.then_inc(s_oT_ps, 1)

            def project(b, i):
                pe.wait_ge(s_oT, b + 1)
                for t in range(T):
                    mm = nc.tensor.matmul(ps[:, O_BANK + i, LQ + D * t:LQ + D * t + D], oT[:, P * t:P * t + P], wo_sb[:, :], start=True, stop=True)
                mm.then_inc(s_wo_ps, 1)

            def rows2_T(c):
                pe.wait_ge(s_xn2, c * 4 + 4)
                for t in range(4):
                    mm = nc.tensor.transpose(ps[:, X2_BANK[c], P * t:P * t + P], xn[:, t, :], ident[:, :])
                mm.then_inc(s_x2_ps, 1)

            def slot(u, b, v, at, n):
                h = v % 2
                if at + 1 < U:
                    shifted(u + 1, (v + 1) // 2 % 2, (v + 1) % 2, True)
                if at + 3 < U:
                    if at >= 1:
                        pe.wait_ge(s_qop[(v + 3) // 2 % 2][1 - h], n * 32 + 32 * ((v + 3) // 4))
                    scores(u + 3, (v + 3) // 2 % 2, 1 - h, True)
                if at + 2 < U:
                    maxima_T(u + 2, h)
                if h == 0 and at >= 4:
                    project(b - 2, v // 2)
                if at >= 1:
                    values(u - 1, b - 1 + h, (v - 1) // 2 % 2, 1 - h, at >= 5)
                if h == 1 and 3 <= at < U - 1:
                    out_T(b - 1, 1 - v // 2)

            pe.wait_ge(s_ctxT, 2)
            pe.wait_ge(s_vset, 1)
            pe.wait_ge(s_rep, 2)
            keys(0)
            bias_rows()
            keys(1)
            rows_T(0)
            keys(2)
            keys(3)
            pe.wait_ge(s_xnT, 1)
            pe.wait_ge(s_bqs, 2)
            for r in range(R):
                first_queries(r)
            pe.wait_ge(s_kl, R)
            pe.wait_ge(s_wv, 32)
            for b in range(B):
                mm = nc.tensor.matmul(ps[:, 2 + b // 4, P * (b % 4):P * (b % 4) + P], ctxT[:, b, :, :].rearrange("p m k -> p (m k)"),
                                      wv_sb[:, :], start=True, stop=True)
            mm.then_inc(s_v_ps, 1)
            pe.wait_ge(s_ql, 1)
            rows_T(1)
            pe.wait_ge(s_ql, 2)
            scores(0, 0, 0, False)
            pe.wait_ge(s_bqs, 4)
            queries(1)
            pe.wait_ge(s_ql, R)
            rows_T(2)
            queries(2)
            maxima_T(0, 0)
            rows_T(3)
            pe.wait_ge(s_ql, R + 1)
            queries(3)
            pe.wait_ge(s_vr, 4)
            scores(1, 0, 1, False)
            pe.wait_ge(s_ql, R + NC - 1)
            shifted(0, 0, 0, False)
            maxima_T(1, 1)
            scores(2, 1, 0, True)
            pe.wait_ge(s_v3, 2)
            pe.wait_ge(s_wo, 16)
            for u in range(4):
                slot(u, u // 2, u, u, 0)
            with pe.Fori(1, U // 4 - 1) as n:
                for v in range(4):
                    slot(n * 4 + v, n * 2 + v // 2, v, 4 + v, n)
            slot(U - 4, B - 2, 0, U - 4, U // 4 - 1)
            slot(U - 3, B - 2, 1, U - 3, U // 4 - 1)
            pe.wait_ge(s_wmax, 1)
            nc.tensor.transpose(ps[0:3, 0, 0:P], wmax[:, :], ident[:, :]).then_inc(s_wmT_ps, 1)
            pe.wait_ge(s_wd, 1)
            nc.tensor.matmul(ps[:, 0, LQ:LQ + 3], ones3[0:3, :], wmaxd[0:3, 0:3], start=True, stop=True).then_inc(s_wb_ps, 1)
            slot(U - 2, B - 1, 2, U - 2, U // 4 - 1)
            rows2_T(0)
            slot(U - 1, B - 1, 3, U - 1, U // 4 - 1)

            def three(dst, m, e, cols, hi, lo, start, stop):
                ws_hi = w16[:, m, bass.ds(e, 1), cols].rearrange("p a c -> p (a c)")
                ws_lo = w16[:, 3 + m, bass.ds(e, 1), cols].rearrange("p a c -> p (a c)")
                nc.tensor.matmul(dst, ws_hi, hi, start=start, stop=False)
                nc.tensor.matmul(dst, ws_hi, lo, start=False, stop=False)
                return nc.tensor.matmul(dst, ws_lo, hi, start=False, stop=stop)

            def gate_up(i, c, e, u, fresh, arriving):
                if arriving:
                    pe.wait_ge(s_wl, e * 3 + 1)
                if not fresh:
                    pe.wait_ge(s_sg, i - 1)
                cols = slice(P * u, P * u + P)
                three(ps[:, u % 2, :], 0, e, cols, xh[:, c, :], xl[:, c, :], True, True).then_inc(s_g, 1)
                if arriving:
                    pe.wait_ge(s_wl, e * 3 + 2)
                if not fresh:
                    pe.wait_ge(s_h, i - 1)
                three(ps[:, 2 + u % 2, :], 1, e, cols, xh[:, c, :], xl[:, c, :], True, True).then_inc(s_u, 1)

            def down(i, e, u, start, stop):
                pe.wait_ge(s_hl, i + 1)
                three(ps[:, 4, :], 2, e, slice(P * u, P * u + P), hh[u], hl[u], start, stop).then_inc(s_d, 1)

            def body(c, e, first=False, arriving=False):
                fresh = c == 0 and first
                for u in range(FT):
                    i = (c * E + e) * FT + u
                    gate_up(i, c, e, u, fresh and u < 2, arriving and u == 0)
                    if fresh and u == 0:
                        out_T(B - 2, 0)
                    if fresh and u == 1:
                        project(B - 2, 0)
                        values(U - 1, B - 1, 1, 1, False)
                    if u < 2:
                        if not fresh:
                            down(i - 2, (E - 1) if first else e - 1, u + 2, False, first and u == 1)
                    else:
                        if first and u == 2 and c > 0:
                            pe.wait_ge(s_yT, c)
                        if arriving and u == 2:
                            pe.wait_ge(s_wl, e * 3 + 3)
                        down(i - 2, e, u - 2, first and u == 2, False)

            def rows_back(c):
                pe.wait_ge(s_yT, c + 1)
                if c > 0:
                    pe.wait_ge(s_y, c)
                for t in range(4):
                    mm = nc.tensor.transpose(ps[:, 6, P * t:P * t + P], yT[:, P * t:P * t + P], ident[:, :])
                mm.then_inc(s_y_ps, 1)

            pe.wait_ge(s_xl, 1)
            for c in range(NC):
                if c > 0:
                    pe.wait_ge(s_xl, c + 1)
                body(c, 0, first=True, arriving=(c == 0))
                if c == 0:
                    out_T(B - 1, 1)
                    project(B - 1, 1)
                if c > 0:
                    rows_back(c - 1)
                with pe.Fori(1, E_MID + 2) as e:
                    body(c, e, arriving=(c == 0))
                if c + 1 < NC:
                    rows2_T(c + 1)
                with pe.Fori(E_MID + 2, E) as e:
                    body(c, e, arriving=(c == 0))
            last = NC * E * FT
            down(last - 2, E - 1, 2, False, False)
            down(last - 1, E - 1, 3, False, True)
            rows_back(NC - 1)


_INS = ["x", "ctx_512", "L0_xattn_Wq", "L0_xattn_bq", "L0_xattn_Wk", "L0_xattn_bk", "L0_xattn_Wv", "L0_xattn_bv",
        "L0_xattn_Wo", "L0_xattn_bo", "L0_ffn_Wg", "L0_ffn_Wu", "L0_ffn_Wd"]


def kernel(**inputs):
    import numpy as np
    import concourse.bacc as bacc
    from concourse.bass_utils import run_bass_kernel_spmd

    nc = bacc.Bacc("TRN2", target_bir_lowering=False, num_devices=1)
    arrays, args = {}, []
    for name in _INS:
        a = np.ascontiguousarray(inputs[name])
        arrays[f"in_{name}"] = a
        args.append(nc.dram_tensor(f"in_{name}", a.shape, mybir.dt.from_np(a.dtype), kind="ExternalInput").ap())
    out = nc.dram_tensor("out_rows", inputs["x"].shape, F32, kind="ExternalOutput").ap()
    build(nc, *args, out)
    r = run_bass_kernel_spmd(nc, [arrays], core_ids=[0])
    return r.results[0]["out_rows"]
```
